# Optimizing a Trainium2 kernel written in Bass

```python
import numpy as np
import jax
import jax.numpy as jnp

def _softmax(x, axis=-1):
    return jax.nn.softmax(x, axis=axis)

def _gelu(x):
    return jax.nn.gelu(x, approximate=True)

def _silu(x):
    return jax.nn.silu(x)

def _sigmoid(x):
    return jax.nn.sigmoid(x)

def _layernorm(x, axis=-1, eps=1e-05):
    m = jnp.mean(x, axis=axis, keepdims=True)
    v = jnp.var(x, axis=axis, keepdims=True)
    return (x - m) / jnp.sqrt(v + eps)

def _scatter_add(tgt, idx, src, axis=0):
    return tgt.at[idx].add(src)

def _segment_sum(src, seg, n):
    return jax.ops.segment_sum(src, seg, n)
kernel_name = 'mk_conv_preact_d2_conv_nchw768_r4_195997'

def setup_inputs(seed: int=0):
    np.random.seed(seed)
    _w = jnp.asarray

    def _rec_inputs():
        import jax
        import jax.numpy as jnp
        _gk = jax.random.key(seed)
        x = -0.0002221 + 1 * jax.random.normal(jax.random.fold_in(_gk, 1), (32, 192, 32, 32), jnp.float32)
        return x
    x = _rec_inputs()

    def _L0_conv_setup():
        import jax, jax.numpy as jnp
        import numpy as np
        IN_DIM = 192
        NUM_HEADS = 4
        SCALE = float((IN_DIM // NUM_HEADS) ** (-0.5))
        key = jax.random.key(seed)
        k1, k2, k3 = jax.random.split(key, 3)
        B, C, H, W = (32, IN_DIM, 32, 32)
        x = jax.random.normal(k1, (B, C, H, W), dtype=jnp.float32)
        w_qkv = jax.random.normal(k2, (3 * C, C), dtype=jnp.float32) * C ** (-0.5)
        w_out = jax.random.normal(k3, (C, C), dtype=jnp.float32) * C ** (-0.5)
        b_out = jnp.zeros((C,), dtype=jnp.float32)
        return {'x': x, 'w_qkv': w_qkv, 'w_out': w_out, 'b_out': b_out}
    _L0_conv_all = _L0_conv_setup()
    _L0_conv_in = {k: v for k, v in _L0_conv_all.items() if k in ('w_qkv', 'w_out', 'b_out')}
    del _L0_conv_all

    def _L1_conv_setup():
        import jax, jax.numpy as jnp
        import numpy as np
        B, C, H, W = (8, 192, 32, 32)
        CO, KS = (192, 3)

        def _conv(x, w, b):
            y = jax.lax.conv_general_dilated(x, w, (1, 1), [(1, 1), (1, 1)], dimension_numbers=('NCHW', 'OIHW', 'NCHW'))
            return y + b[None, :, None, None]

        def _deform_conv(x, offset, mask, w, b):
            b_, c_, h_, w_ = x.shape
            co, _, kh, kw = w.shape
            K = kh * kw
            off = offset.reshape(b_, K, 2, h_, w_)
            ky = (jnp.arange(K) // kw).astype(x.dtype)
            kx = (jnp.arange(K) % kw).astype(x.dtype)
            py = off[:, :, 0] + (jnp.arange(h_, dtype=x.dtype) - 1.0)[None, None, :, None] + ky[None, :, None, None]
            px = off[:, :, 1] + (jnp.arange(w_, dtype=x.dtype) - 1.0)[None, None, None, :] + kx[None, :, None, None]
            y0 = jnp.floor(py)
            x0 = jnp.floor(px)
            wy1 = py - y0
            wx1 = px - x0
            y0i = y0.astype(jnp.int32)
            x0i = x0.astype(jnp.int32)

            def corner(yi, xi, wt):
                valid = (yi >= 0) & (yi < h_) & (xi >= 0) & (xi < w_)
                yc = jnp.clip(yi, 0, h_ - 1)
                xc = jnp.clip(xi, 0, w_ - 1)
                g = jax.vmap(lambda im, yy, xx: im[:, yy, xx])(x, yc, xc)
                return g * (wt * valid)[:, None]
            p = corner(y0i, x0i, (1.0 - wy1) * (1.0 - wx1) * mask) + corner(y0i, x0i + 1, (1.0 - wy1) * wx1 * mask) + corner(y0i + 1, x0i, wy1 * (1.0 - wx1) * mask) + corner(y0i + 1, x0i + 1, wy1 * wx1 * mask)
            out = jnp.einsum('bckhw,ock->bohw', p, w.reshape(co, c_, K))
            return out + b[None, :, None, None]
        key = jax.random.key(seed)
        ks = jax.random.split(key, 6)
        x = jax.random.normal(ks[0], (B, C, H, W), jnp.float32)
        proj_w = jax.random.normal(ks[1], (CO, C, KS, KS), jnp.float32) * 0.02
        proj_b = jnp.zeros((CO,), jnp.float32)
        off_w = jax.random.normal(ks[2], (2 * KS * KS, C, KS, KS), jnp.float32) * 0.01
        off_b = jax.random.normal(ks[3], (2 * KS * KS,), jnp.float32) * 0.01
        mask_w = jax.random.normal(ks[4], (KS * KS, C, KS, KS), jnp.float32) * 0.01
        mask_b = jax.random.normal(ks[5], (KS * KS,), jnp.float32) * 0.01
        gamma = jnp.ones((CO,), jnp.float32)
        beta = jnp.zeros((CO,), jnp.float32)
        return {'x': x, 'proj_w': proj_w, 'proj_b': proj_b, 'off_w': off_w, 'off_b': off_b, 'mask_w': mask_w, 'mask_b': mask_b, 'gamma': gamma, 'beta': beta}
    _L1_conv_all = _L1_conv_setup()
    _L1_conv_in = {k: v for k, v in _L1_conv_all.items() if k in ('proj_w', 'proj_b', 'off_w', 'off_b', 'mask_w', 'mask_b', 'gamma', 'beta')}
    del _L1_conv_all
    return {'x': x, 'L0_conv_w_qkv': _L0_conv_in['w_qkv'], 'L0_conv_w_out': _L0_conv_in['w_out'], 'L0_conv_b_out': _L0_conv_in['b_out'], 'L1_conv_proj_w': _L1_conv_in['proj_w'], 'L1_conv_proj_b': _L1_conv_in['proj_b'], 'L1_conv_off_w': _L1_conv_in['off_w'], 'L1_conv_off_b': _L1_conv_in['off_b'], 'L1_conv_mask_w': _L1_conv_in['mask_w'], 'L1_conv_mask_b': _L1_conv_in['mask_b'], 'L1_conv_gamma': _L1_conv_in['gamma'], 'L1_conv_beta': _L1_conv_in['beta']}

def reference(x, L0_conv_w_qkv, L0_conv_w_out, L0_conv_b_out, L1_conv_proj_w, L1_conv_proj_b, L1_conv_off_w, L1_conv_off_b, L1_conv_mask_w, L1_conv_mask_b, L1_conv_gamma, L1_conv_beta):
    import jax
    import jax.numpy as jnp

    def _L0_conv_ref(x, w_qkv, w_out, b_out):
        import jax, jax.numpy as jnp
        import numpy as np
        IN_DIM = 192
        NUM_HEADS = 4
        SCALE = float((IN_DIM // NUM_HEADS) ** (-0.5))
        B, C, H, W = x.shape
        N = H * W
        x_flat = x.reshape(B, C, N).transpose(0, 2, 1)
        qkv = jnp.einsum('bnc,dc->bnd', x_flat, w_qkv)
        q, k, v = jnp.split(qkv, 3, axis=-1)
        q = q.transpose(0, 2, 1)
        k = k.transpose(0, 2, 1)
        v = v.transpose(0, 2, 1)
        attn = jnp.einsum('bcn,bdn->bcd', q, k) * SCALE
        attn = jax.nn.softmax(attn, axis=-1)
        out = jnp.einsum('bcd,bdn->bcn', attn, v)
        out = out.transpose(0, 2, 1)
        out = jnp.einsum('bnc,dc->bnd', out, w_out) + b_out
        out = out.transpose(0, 2, 1).reshape(B, C, H, W)
        return out

    def _L1_conv_ref(x, proj_w, proj_b, off_w, off_b, mask_w, mask_b, gamma, beta):
        import jax, jax.numpy as jnp
        import numpy as np
        B, C, H, W = (8, 192, 32, 32)
        CO, KS = (192, 3)

        def _conv(x, w, b):
            y = jax.lax.conv_general_dilated(x, w, (1, 1), [(1, 1), (1, 1)], dimension_numbers=('NCHW', 'OIHW', 'NCHW'))
            return y + b[None, :, None, None]

        def _deform_conv(x, offset, mask, w, b):
            b_, c_, h_, w_ = x.shape
            co, _, kh, kw = w.shape
            K = kh * kw
            off = offset.reshape(b_, K, 2, h_, w_)
            ky = (jnp.arange(K) // kw).astype(x.dtype)
            kx = (jnp.arange(K) % kw).astype(x.dtype)
            py = off[:, :, 0] + (jnp.arange(h_, dtype=x.dtype) - 1.0)[None, None, :, None] + ky[None, :, None, None]
            px = off[:, :, 1] + (jnp.arange(w_, dtype=x.dtype) - 1.0)[None, None, None, :] + kx[None, :, None, None]
            y0 = jnp.floor(py)
            x0 = jnp.floor(px)
            wy1 = py - y0
            wx1 = px - x0
            y0i = y0.astype(jnp.int32)
            x0i = x0.astype(jnp.int32)

            def corner(yi, xi, wt):
                valid = (yi >= 0) & (yi < h_) & (xi >= 0) & (xi < w_)
                yc = jnp.clip(yi, 0, h_ - 1)
                xc = jnp.clip(xi, 0, w_ - 1)
                g = jax.vmap(lambda im, yy, xx: im[:, yy, xx])(x, yc, xc)
                return g * (wt * valid)[:, None]
            p = corner(y0i, x0i, (1.0 - wy1) * (1.0 - wx1) * mask) + corner(y0i, x0i + 1, (1.0 - wy1) * wx1 * mask) + corner(y0i + 1, x0i, wy1 * (1.0 - wx1) * mask) + corner(y0i + 1, x0i + 1, wy1 * wx1 * mask)
            out = jnp.einsum('bckhw,ock->bohw', p, w.reshape(co, c_, K))
            return out + b[None, :, None, None]
        h, w = (x.shape[-2], x.shape[-1])
        max_off = float(min(h, w) // 4)
        offset = jnp.clip(_conv(x, off_w, off_b), -max_off, max_off)
        mask = 2.0 * jax.nn.sigmoid(_conv(x, mask_w, mask_b))
        y = _deform_conv(x, offset, mask, proj_w, proj_b)
        mean = y.mean(axis=(0, 2, 3))
        var = y.var(axis=(0, 2, 3))
        yn = (y - mean[None, :, None, None]) * jax.lax.rsqrt(var + 1e-05)[None, :, None, None]
        yn = yn * gamma[None, :, None, None] + beta[None, :, None, None]
        return jax.nn.gelu(yn, approximate=False)

    def _gn(v, G=32, eps=1e-05):
        B_, C_, H_, W_ = v.shape
        g = v.reshape(B_, G, C_ // G, H_, W_)
        m = jnp.mean(g, axis=(2, 3, 4), keepdims=True)
        s = jnp.var(g, axis=(2, 3, 4), keepdims=True)
        return ((g - m) / jnp.sqrt(s + eps)).reshape(v.shape)

    def _ln_c(v, eps=1e-06):
        m = jnp.mean(v, axis=1, keepdims=True)
        s = jnp.var(v, axis=1, keepdims=True)
        return (v - m) / jnp.sqrt(s + eps)

    def _ln_t(v, eps=1e-05):
        m = jnp.mean(v, axis=-1, keepdims=True)
        s = jnp.var(v, axis=-1, keepdims=True)
        return (v - m) / jnp.sqrt(s + eps)

    def _to_tokens(v):
        B_, C_, H_, W_ = v.shape
        return v.reshape(B_, C_, H_ * W_).transpose(0, 2, 1)

    def _from_tokens(t, like):
        B_, C_, H_, W_ = like.shape
        return t.transpose(0, 2, 1).reshape(B_, C_, H_, W_)
    x = x + _L0_conv_ref(_gn(x), L0_conv_w_qkv, L0_conv_w_out, L0_conv_b_out)
    x = x + _L1_conv_ref(_gn(x), L1_conv_proj_w, L1_conv_proj_b, L1_conv_off_w, L1_conv_off_b, L1_conv_mask_w, L1_conv_mask_b, L1_conv_gamma, L1_conv_beta)
    return x

_drawn_inputs = setup_inputs


def setup_inputs(seed=0):
    import zlib

    import numpy as np

    out = dict(_drawn_inputs(seed))
    spreads = {'L0_conv_b_out': (0.0, 0.1),
     'L1_conv_proj_b': (0.0, 0.8),
     'L1_conv_gamma': (1.0, 0.2),
     'L1_conv_beta': (0.0, 0.1)}
    factors = {'L1_conv_off_b': 4.034}
    for name, (base, spread) in spreads.items():
        noise = np.random.default_rng([zlib.crc32(name.encode()), seed]).standard_normal(out[name].shape)
        drawn = base * np.exp(spread * noise) if base else spread * noise
        out[name] = jnp.asarray(drawn.astype(out[name].dtype))
    for name, factor in factors.items():
        out[name] = (out[name] * factor).astype(out[name].dtype)
    return out
```

```python
from contextlib import ExitStack

import numpy as np
import concourse.bass as bass
from concourse import mybir

F32, F16, I32 = mybir.dt.float32, mybir.dt.float16, mybir.dt.int32
ALU = mybir.AluOpType
ACT = mybir.ActivationFunctionType
AX = mybir.AxisListType

P = 128
C, H, W = 192, 32, 32
N = H * W
CB = C - P
TAPS = 9
J = 3 * TAPS
GROUPS = 32
ROWS_T = P // W
TILES = N // P
CHUNKS = TILES + 1
R = 2 * ROWS_T
CENTRE = (R - 1) / 2
MAX_OFF = float(min(H, W) // 4)
PAD_T, PAD_ROWS = 3, 40
KO = 3 * C
UNITS = 6 * TILES
HEAD_SCALE = float((C // 4) ** (-0.5))
GN_EPS = 1e-5
BN_EPS = 1e-5
FAR = [-2, -1, 2, 3]


def coordinate_tables():
    c = np.concatenate([np.arange(P), np.arange(P, C), np.arange(P, C)])
    g = c // (C // GROUPS)
    avg = np.zeros((P, 4, P), np.float32)
    for fb in range(2):
        for tb in range(2):
            same = g[fb * P:fb * P + P, None] == g[None, tb * P:tb * P + P]
            avg[:, 2 * fb + tb, :] = same * np.float32(1.0 / (C // GROUPS))
    p = np.arange(P)
    rows_near = np.arange(R)
    rows_far = np.concatenate([np.arange(ROWS_T) + ROWS_T * f for f in FAR])
    cy = (p[:, None] // W + 2 - np.concatenate([rows_near, rows_far])[None, :]).astype(np.float32)
    k = np.arange(TAPS)
    cx = (p[:, None, None] % W - 1 + (k % 3)[None, :, None] - np.arange(W)[None, None, :]).astype(np.float32)
    return avg.reshape(P, -1), cy, cx.reshape(P, -1), np.eye(P, dtype=np.float32)


def build(nc, x, w_qkT, w_v, w_outT, b_out, w_off, b_off, w_proj, proj_b, gamma, beta,
          avg, cy, cx, eye, out):
    NB = x.shape[0]
    nc.disable_value_cache = True
    x1_dram = nc.dram_tensor("x1_scratch", [NB, C, N], F32, kind="Internal").ap()
    y_dram = nc.dram_tensor("y_scratch", [NB, C, N], F32, kind="Internal").ap()

    with ExitStack() as ctx:
        def sb(name, shape, dt=F32):
            return ctx.enter_context(nc.sbuf_tensor(name, shape, dt))

        def bank(name, shape=(P, 512), dt=F32):
            return ctx.enter_context(nc.psum_tensor(name, list(shape), dt))

        def sem(name):
            return ctx.enter_context(nc.semaphore(name))

        avg_sb = sb("avg_sb", [P, 4, P])
        cy_sb = sb("cy_sb", [P, R + 4 * len(FAR)])
        cx_sb = sb("cx_sb", [P, TAPS, W])
        eye32 = sb("eye32", [P, P])
        eye16 = sb("eye16", [P, P], F16)
        mhalf = sb("mhalf", [P, 2])
        minus = sb("minus", [P, 2])
        wqk = sb("wqk", [P, 2, 2 * C])
        wv = sb("wv", [P, 2, 2 * P])
        wo = sb("wo", [P, 2, 2 * P])
        wof_h = sb("wof_h", [P, 2, TAPS, J], F16)
        wof_l = sb("wof_l", [P, 2, TAPS, J], F16)
        wpr_h = sb("wpr_h", [P, 2, 3, KO], F16)
        wpr_l = sb("wpr_l", [P, 2, 3, KO], F16)
        bo = sb("bo", [P, 2])
        pb = sb("pb", [P, 2])
        gam = sb("gam", [P, 2])
        bet = sb("bet", [P, 2])
        boff = sb("boff", [P, TILES, J])
        wmax = sb("wmax", [P, 2])
        wmaxt = sb("wmaxt", [P, 2])
        unscale = sb("unscale", [P, 2])
        scale = sb("scale", [P, 2])
        xin = sb("xin", [P, 2, N])
        xn = sb("xn", [P, 2, N])
        x1 = sb("x1", [P, 2, N])
        stats = sb("stats", [P, 2, 2, 6])
        mv = sb("mv", [P, 2, 2])
        msq = sb("msq", [P, 2])
        gmv = sb("gmv", [P, 2, 2])
        gvar = sb("gvar", [P, 2])
        rstd = sb("rstd", [P, 2])
        nbias = sb("nbias", [P, 2])
        xh_a = sb("xh_a", [P, N], F16)
        xl_a = sb("xl_a", [P, N], F16)
        xhl_b = sb("xhl_b", [P, N], F16)
        xt = sb("xt", [P, TILES, 2 * C], F16)
        gram = sb("gram", [P, 2, C])
        t1 = sb("t1", [P, 2, C])
        prob = sb("prob", [P, 2, C])
        rmat = sb("rmat", [P, 2, 2 * P])
        mt_h = sb("mt_h", [P, 2, 2 * P], F16)
        mt_l = sb("mt_l", [P, 2, 2 * P], F16)
        nmax = sb("nmax", [P, 2])
        nmaxs = sb("nmaxs", [P, 2])
        rsum = sb("rsum", [P, 2])
        rinv = sb("rinv", [P, 2])
        x2s = [sb(f"x2s_{n}", [P, 2, PAD_ROWS * W], F16) for n in ("hi_a", "lo_a", "hilo_b")]
        x2 = [sb(f"x2_{n}", [P, 2, PAD_ROWS * W], F16) for n in ("hi_a", "lo_a", "hilo_b")]
        off = sb("off", [P, 2, TILES, J])
        ay = sb("ay", [P, 2, TILES * TAPS, R])
        bx = sb("bx", [P, 2, TILES * TAPS, W])
        mask = sb("mask", [P, 2, TILES, TAPS])
        cmid = sb("cmid", [P, 1])
        ypos = sb("ypos", [P, TILES, TAPS])
        offmax = sb("offmax", [P, 1])
        offmaxg = sb("offmaxg", [P, 1])
        far = sb("far", [P, 2], I32)
        Z_RING = 6
        zh = sb("zh", [P, Z_RING, 3, KO], F16)
        zl = sb("zl", [P, Z_RING, 3, KO], F16)
        ST_RING = 3
        sT = sb("sT", [P, ST_RING, 3, R * W])
        S_RING = 3
        sh = sb("sh", [P, S_RING, 3, P], F16)
        sl = sb("sl", [P, S_RING, 3, P], F16)
        ypm = sb("ypm", [P, 4, 2 * P])
        ych = sb("ych", [P, 2, 2, N])
        ystats = sb("ystats", [P, 2, NB * 2, 6])
        ymv = sb("ymv", [P, 2, 2])
        yvar = sb("yvar", [P, 2])
        yrstd = sb("yrstd", [P, 2])
        ga = sb("ga", [P, 2])
        gmean = sb("gmean", [P, 2])
        gb = sb("gb", [P, 2])

        acc = bank("acc")
        yt = bank("yt")
        zps = bank("zps", (P, 2, 512))
        sps = [bank(f"sps{i}") for i in range(2)]
        l0 = [bank(f"l0_{i}") for i in range(2)]

        const_in = sem("const_in")
        dve_setup = sem("dve_setup")
        pool_setup = sem("pool_setup")
        pe_setup = sem("pe_setup")
        act_setup = sem("act_setup")
        x_loaded = sem("x_loaded")
        gn_stats = sem("gn_stats")
        gn_group = sem("gn_group")
        gn_var = sem("gn_var")
        gn_rstd = sem("gn_rstd")
        gn_mean = sem("gn_mean")
        gn_bias = sem("gn_bias")
        xn_hi = sem("xn_hi")
        xn_lo = sem("xn_lo")
        xt_ps = sem("xt_ps")
        xt_sb = sem("xt_sb")
        gram_ps = sem("gram_ps")
        gram_sb = sem("gram_sb")
        t1_ps = sem("t1_ps")
        t1_sb = sem("t1_sb")
        log_ps = sem("log_ps")
        log_max = sem("log_max")
        prob_exp = sem("prob_exp")
        prob_sb = sem("prob_sb")
        r_ps = sem("r_ps")
        r_sb = sem("r_sb")
        mt_ps = sem("mt_ps")
        mt_hi = sem("mt_hi")
        mt_lo = sem("mt_lo")
        mx_ps = sem("mx_ps")
        x1_sb = sem("x1_sb")
        x1_stored = sem("x1_stored")
        x2_moved = sem("x2_moved")
        off_ps = sem("off_ps")
        off_sb = sem("off_sb")
        d_sb = sem("d_sb")
        hat_act = sem("hat_act")
        hats = sem("hats")
        omax_sb = sem("omax_sb")
        omax_ps = sem("omax_ps")
        flag_sb = sem("flag_sb")
        z_ps = sem("z_ps")
        z_hi = sem("z_hi")
        z_lo = sem("z_lo")
        st_made = sem("st_made")
        s_ps = sem("s_ps")
        s_hi = sem("s_hi")
        s_lo = sem("s_lo")
        sz_done = sem("sz_done")
        y_pm = sem("y_pm")
        yt_ps = sem("yt_ps")
        y_ch = sem("y_ch")
        y_final = sem("y_final")
        y_free = [sem(f"y_free{i}") for i in range(2)]
        fz_ps = sem("fz_ps")
        fz_hi = sem("fz_hi")
        fz_lo = sem("fz_lo")
        f_st = sem("f_st")
        fs_ps = sem("fs_ps")
        fs_hi = sem("fs_hi")
        fs_lo = sem("fs_lo")
        fsz_done = sem("fsz_done")
        fy_pm = sem("fy_pm")
        fyt_ps = sem("fyt_ps")
        fy_ch = sem("fy_ch")
        flag_seen = sem("flag_seen")
        far_left = sem("far_left")
        bn_var = sem("bn_var")
        bn_rstd = sem("bn_rstd")
        bn_done = sem("bn_done")
        f_loaded = [sem(f"f_loaded{i}") for i in range(2)]
        f_gelu = sem("f_gelu")
        f_sum = sem("f_sum")
        f_stored = [sem(f"f_stored{i}") for i in range(2)]

        ZG = 3 * CHUNKS
        SLOTS = UNITS
        CONST_DMAS = 4 + TILES + 3 + 8 + 3 * 4 + 3 + 3

        def flat(t):
            v = t[tuple([slice(None)] * len(t.shape))]
            return v.rearrange("p a b -> p (a b)")

        def flat2(t):
            v = t[:, :, :, :]
            return v.rearrange("p i a b -> p i (a b)")

        def hat4(t, par, n):
            return t[:, par].rearrange("p (t k) n -> p t k n", t=TILES)

        def spread(v, n):
            return v[:, :, :, None].broadcast_to([P, TILES, TAPS, n])

        zl_flat = zl[:, :, :, :].rearrange("p j k o -> p (j k o)")
        zh_flat = zh[:, :, :, :].rearrange("p j k o -> p (j k o)")
        proj_stage = zl_flat[:, 0:2 * 2 * TAPS * C].bitcast(F32).rearrange("p (i n) -> p i n", i=2)
        off_stage = zh_flat[:, 0:2 * 2 * TAPS * J].bitcast(F32).rearrange("p (i n) -> p i n", i=2)
        ayf = xn[:, :, :].rearrange("p a n -> p (a n)")[:, 0:TILES * TAPS * 4 * ROWS_T]\
            .rearrange("p (k r) -> p k r", r=4 * ROWS_T)
        sTf = xt[:, :, :].rearrange("p t n -> p (t n)").bitcast(F32).rearrange("p (k m) -> p k m", k=3)
        three = lambda v: v[:, 0:3 * N].rearrange("p (i n) -> p i n", i=3)
        fin_y = [three(v[:, 0:2 * 3 * N].bitcast(F32)) for v in (zh_flat, zl_flat)]
        fin_x = [three(ych[:, :, :, :].rearrange("p a b n -> p (a b n)")),
                 three(bx[:, :, :, :].rearrange("p a k x -> p (a k x)"))]

        def images(program, eng):
            part0, part1 = program
            for u in range(SLOTS):
                part0(u, 0, 0)
            part1(0, 0, True)
            with eng.Fori(1, NB - 2, 2) as b:
                part1(b, 1, True)
                part1(b + 1, 0, True)
            part1(NB - 1, (NB - 1) % 2, False)

        far_units = [(t, ky, f) for t in range(TILES) for ky in range(3)
                     for f, c in enumerate(FAR) if 0 <= t + c < CHUNKS]
        FAR_UNITS = len(far_units)
        far_of = lambda t, ky: [v for v, w in enumerate(far_units) if w[0:2] == (t, ky)]
        far_end = lambda t: sum(w[0] <= t for w in far_units)
        FAR_ROWS = ROWS_T * len(FAR)

        def far_chunks(t):
            return range(0, FAR[-1] + 1) if t == 0 else range(t + FAR[-1], min(t + FAR[-1] + 1, CHUNKS))

        def first(b):
            return isinstance(b, int) and b == 0

        ROWS = (P, CB)
        COLS = (slice(0, P), slice(P, C))

        def where_far(eng, b, par, far_pass, *counts):
            eng.wait_ge(flag_sb, b + 1)
            eng.sem_inc(flag_seen, 1)
            flag = eng.value_load(far[0:1, par:par + 1], min_val=0, max_val=1)
            with eng.If(flag == 1):
                far_pass(b, par)
                eng.sem_inc(far_left, 1)
            with eng.Else():
                for s, n in counts:
                    eng.sem_inc(s, n)

        block = ctx.enter_context(nc.Block())

        @block.sync
        def _(sp):
            def load_blocks(dst, src):
                sp.dma_start(dst[:, 0], src[0:P]).then_inc(const_in, 16)
                sp.dma_start(dst[0:CB, 1], src[P:C]).then_inc(const_in, 16)
                sp.dma_start(dst[CB:P, 1], src[P:C]).then_inc(const_in, 16)

            def load_x(b):
                for dst, src in ((xin[:, 0], x[b, 0:P]), (xin[0:CB, 1], x[b, P:C]), (xin[CB:P, 1], x[b, P:C])):
                    sp.dma_start(dst, src).then_inc(x_loaded, 16)

            for par in range(2):
                sp.sem_inc(y_free[par], 32)
            load_x(0)
            sp.dma_start(avg_sb[:, :, :], avg.rearrange("p (a b) -> p a b", a=4)).then_inc(const_in, 16)
            sp.dma_start(cy_sb[:, :], cy).then_inc(const_in, 16)
            sp.dma_start(cx_sb[:, :, :], cx.rearrange("p (k x) -> p k x", k=TAPS)).then_inc(const_in, 16)
            sp.dma_start(eye32[:, :], eye).then_inc(const_in, 16)
            for t in range(TILES):
                sp.dma_start(boff[:, t, :], b_off.partition_broadcast(P)).then_inc(const_in, 16)
            load_blocks(wqk, w_qkT)
            for dst, src in ((wo, w_outT), (wv, w_v)):
                for i in range(2):
                    rows = slice(i * P, i * P + ROWS[i])
                    sp.dma_start(dst[0:ROWS[i], i, 0:C], src[rows]).then_inc(const_in, 16)
                    sp.dma_start(dst[0:ROWS[i], i, C:2 * P], src[rows, P:C]).then_inc(const_in, 16)
            for dst, src in ((bo, b_out), (pb, proj_b), (gam, gamma), (bet, beta)):
                load_blocks(dst[:, :, None], src[:, None])
            load_blocks(off_stage, w_off)
            load_blocks(proj_stage, w_proj)

            def attended(b, more=True):
                sp.wait_ge(x1_sb, 4 * b + 4)
                sp.dma_start(x1_dram[b, 0:P], x1[:, 0]).then_inc(x1_stored, 16)
                sp.dma_start(x1_dram[b, P:C], x1[0:CB, 1]).then_inc(x1_stored, 16)
                if more:
                    load_x(b + 1)

            def convolved(b, par):
                sp.wait_ge(y_final, b + 1)
                sp.dma_start(y_dram[b, 0:P], ych[:, par, 0]).then_inc(y_free[par], 16)
                sp.dma_start(y_dram[b, P:C], ych[0:CB, par, 1]).then_inc(y_free[par], 16)

            attended(0)
            with sp.Fori(1, NB - 2, 2) as b:
                attended(b)
                convolved(b - 1, 0)
                attended(b + 1)
                convolved(b, 1)
            attended(NB - 1, False)
            convolved(NB - 2, 0)
            convolved(NB - 1, 1)

            sp.wait_ge(x1_stored, 32 * NB)
            for par in range(2):
                sp.wait_ge(y_free[par], 32 + 16 * NB)

            def load_pair(q, slot):
                for dst, src in ((fin_y, y_dram), (fin_x, x1_dram)):
                    for i in range(2):
                        sp.dma_start(dst[slot][:, i], src[2 * q + i, 0:P]).then_inc(f_loaded[slot], 16)
                        sp.dma_start(dst[slot][CB * i:CB * i + CB, 2], src[2 * q + i, P:C]).then_inc(f_loaded[slot], 16)

            sp.wait_ge(bn_var, 1)
            for q in range(2):
                load_pair(q, q)
            with sp.Fori(2, NB // 2 - 1, 2) as q:
                for i in range(2):
                    sp.wait_ge(f_stored[i], 32 * q)
                    load_pair(q + i, i)

        @block.tensor
        def _(pe):
            pe.wait_ge(const_in, CONST_DMAS * 16)
            pe.wait_ge(dve_setup, 1)
            for i in range(2):
                mm = pe.transpose(l0[0][:, i * P:(i + 1) * P], wmax[:, i:i + 1].broadcast_to([P, P]), eye32[:, :])
            mm.then_inc(pe_setup, 1)
            pe.wait_ge(dve_setup, 2)
            pe.wait_ge(pool_setup, 1)

            def group_stats(n, b):
                pe.wait_ge(gn_stats, 2 * b + n + 1)
                for tb in range(2):
                    o = l0[0][:, 2 * tb:2 * tb + 2]
                    pe.matmul(o, avg_sb[:, tb, :], mv[:, 0, :], start=True, stop=False)
                    mm = pe.matmul(o, avg_sb[0:CB, 2 + tb, :], mv[0:CB, 1, :], start=False, stop=True)
                mm.then_inc(gn_group, 1)

            def square(done, lhs, rhs, ps, n):
                for m in range(2):
                    o = ps[0:ROWS[m], m * n:(m + 1) * n]
                    pe.matmul(o, lhs[:, 0, COLS[m]], rhs[:, 0], start=True, stop=False)
                    mm = pe.matmul(o, lhs[0:CB, 1, COLS[m]], rhs[0:CB, 1], start=False, stop=True)
                mm.then_inc(done, 1)

            def transpose_x(r, b):
                if r == 0:
                    pe.wait_ge(xn_lo, 4 * b + 2)
                if r >= 2:
                    pe.wait_ge(xt_sb, 4 * b + r - 1)
                o = l0[r % 2][:, :].bitcast(F16)
                for i in range(2):
                    n = slice((2 * r + i) * P, (2 * r + i + 1) * P)
                    for k, src in enumerate((xh_a, xhl_b, xl_a)):
                        mm = pe.transpose(o[:, i * 3 * P + k * P:i * 3 * P + (k + 1) * P], src[:, n], eye16[:, :])
                mm.then_inc(xt_ps, 1)

            def gram_product(b):
                pe.wait_ge(xt_sb, 4 * b + 4)
                for m in range(2):
                    for t in range(TILES):
                        hi, lo_b, lo_a = xt[:, t, 0:C], xt[:, t, C:2 * P], xt[:, t, 2 * P:3 * P]
                        o = l0[0][0:ROWS[m], m * C:(m + 1) * C]
                        h_m = hi[:, COLS[m]]
                        l_m = (lo_a, lo_b)[m]
                        pe.matmul(o, h_m, hi, start=(t == 0), stop=False)
                        pe.matmul(o[:, 0:P], h_m, lo_a, start=False, stop=False)
                        pe.matmul(o[:, P:C], h_m, lo_b, start=False, stop=False)
                        mm = pe.matmul(o, l_m, hi, start=False, stop=(t == TILES - 1))
                mm.then_inc(gram_ps, 1)

            def apply_m(q, b):
                m, half = divmod(q, 2)
                if q == 0:
                    pe.wait_ge(mt_lo, b + 1)
                if q >= 2:
                    pe.wait_ge(x1_sb, 4 * b + q - 1)
                o = l0[(q + 1) % 2][:, :]
                n = slice(half * 512, half * 512 + 512)
                pe.matmul(o, mt_h[:, 0, m * P:(m + 1) * P], xh_a[:, n], start=True, stop=False)
                pe.matmul(o, mt_h[:, 0, m * P:(m + 1) * P], xl_a[:, n], start=False, stop=False)
                pe.matmul(o, mt_l[:, 0, m * P:(m + 1) * P], xh_a[:, n], start=False, stop=False)
                pe.matmul(o, mt_h[:, 1, m * P:(m + 1) * P], xhl_b[:, n], start=False, stop=False)
                pe.matmul(o, mt_l[:, 1, m * P:(m + 1) * P], xhl_b[:, n], start=False, stop=True).then_inc(mx_ps, 1)

            def window_product(o, par, row, col, w_h, w_l):
                def at(t):
                    plane = x2[t][:, par] if col == 1 else x2s[t][:, col // 2]
                    return plane[:, row * W:(row + ROWS_T) * W]
                pe.matmul(o, at(0), w_h[:, 0], start=o_first[0], stop=False)
                o_first[0] = False
                pe.matmul(o, at(0), w_l[:, 0], start=False, stop=False)
                pe.matmul(o, at(1), w_h[:, 0], start=False, stop=False)
                pe.matmul(o, at(2), w_h[:, 1], start=False, stop=False)
                return lambda last: pe.matmul(o, at(2), w_l[:, 1], start=False, stop=last)

            o_first = [True]

            def offset_conv(t, b, par):
                if t == 0:
                    pe.wait_ge(x2_moved, b + 1)
                o = l0[1][:, t * J:(t + 1) * J]
                o_first[0] = True
                for k in range(TAPS):
                    fin = window_product(o, par, ROWS_T * t + k // 3 - 1 + PAD_T, k % 3,
                                         wof_h[:, :, k], wof_l[:, :, k])
                    mm = fin(k == TAPS - 1)
                if t == TILES - 1:
                    mm.then_inc(off_ps, 1)

            def offset_max(b):
                pe.wait_ge(omax_sb, b + 1)
                pe.transpose(l0[0][:, 0:P], offmax[:, :].broadcast_to([P, P]), eye32[:, :]).then_inc(omax_ps, 1)

            def part0(u, b, par):
                if u == 2:
                    group_stats(0, b)
                if 8 <= u < 12:
                    transpose_x(u - 8, b)
                if u == 13:
                    gram_product(b)
                if u == 15:
                    pe.wait_ge(gram_sb, b + 1)
                    square(t1_ps, gram, wq, l0[1], C)
                if u == 17:
                    pe.wait_ge(t1_sb, b + 1)
                    square(log_ps, t1, wk, l0[0], C)
                if u == 20:
                    pe.wait_ge(prob_sb, b + 1)
                    square(r_ps, prob, wo, l0[1], 2 * P)
                if u == 22:
                    pe.wait_ge(r_sb, b + 1)
                    for m in range(2):
                        o = l0[0][:, m * 2 * P:(m + 1) * 2 * P]
                        pe.matmul(o, wv[:, 0, m * P:(m + 1) * P], rmat[:, 0], start=True, stop=False)
                        mm = pe.matmul(o, wv[0:CB, 1, m * P:(m + 1) * P], rmat[0:CB, 1], start=False, stop=True)
                    mm.then_inc(mt_ps, 1)
                if 24 <= u < 28:
                    apply_m(u - 24, b)
                if u == 30:
                    group_stats(1, b)
                if 36 <= u < 44:
                    offset_conv(u - 36, b, par)
                if u == 46:
                    offset_max(b)

            def z_group(g, b, par):
                if g > 0 or not first(b):
                    pe.wait_ge(z_lo, ZG * b + g)
                z_product(g, par).then_inc(z_ps, 1)

            def z_product(g, par):
                j, ky = divmod(g, 3)
                for half in range(2):
                    o = zps[:, half, 0:KO // 2]
                    cols = slice(half * KO // 2, (half + 1) * KO // 2)
                    o_first[0] = True
                    mm = window_product(o, par, ROWS_T * j + ky, 1, wpr_h[:, :, ky, cols],
                                        wpr_l[:, :, ky, cols])(True)
                return mm

            def turn_s(u, b):
                t, ky, c = u // 6, u % 6 // 2, u % 2
                if c == 0:
                    pe.wait_ge(st_made, 24 * b + 3 * t + ky + 1)
                if u >= 2 or not first(b):
                    pe.wait_ge(s_lo, UNITS * b + u - 1)
                g = (3 * t + ky) % ST_RING
                for kx in range(3):
                    mm = pe.transpose(sps[u % 2][:, kx * P:(kx + 1) * P], sT[:, g, kx, c * P:(c + 1) * P], eye32[:, :])
                mm.then_inc(s_ps, 1)

            def convolve(u, b):
                t, ky, c = u // 6, u % 6 // 2, u % 2
                pe.wait_ge(s_lo, UNITS * b + u + 1)
                if c == 1 or t == 0:
                    pe.wait_ge(z_lo, ZG * b + 3 * (t + c) + ky + 1)
                if u % 6 == 0 and (t > 0 or not first(b)):
                    pe.wait_ge(y_pm, TILES * b + t)
                s_product(u, (t + c) % Z_RING, ky, u % 6 == 0, u % 6 == 5).then_inc(sz_done, 1)

            def s_product(u, j, ky, start, stop):
                for kx in range(3):
                    z = slice(kx * C, (kx + 1) * C)
                    s_h, s_l = sh[:, u % S_RING, kx], sl[:, u % S_RING, kx]
                    pe.matmul(acc[:, 0:C], s_h, zh[:, j, ky, z], start=start and kx == 0, stop=False)
                    pe.matmul(acc[:, 0:C], s_h, zl[:, j, ky, z], start=False, stop=False)
                    mm = pe.matmul(acc[:, 0:C], s_l, zh[:, j, ky, z], start=False, stop=stop and kx == 2)
                return mm

            def turn_y(q, b):
                pe.wait_ge(y_pm, TILES * b + 2 * q + 2)
                if q > 0 or not first(b):
                    pe.wait_ge(y_ch, 4 * b + q)
                for i in range(2):
                    y = ypm[:, (2 * q + i) % 4]
                    pe.transpose(yt[:, i * P:(i + 1) * P], y[:, 0:P], eye32[:, :])
                    mm = pe.transpose(yt[:, (2 + i) * P:(3 + i) * P], y[:, P:2 * P], eye32[:, :])
                mm.then_inc(yt_ps, 1)

            def far_pass(b, par):
                pe.wait_ge(s_lo, UNITS * (b + 1))
                pe.wait_ge(z_lo, ZG * (b + 1))
                pe.wait_ge(y_ch, 4 * (b + 1))
                pe.wait_ge(y_pm, TILES * (b + 1))
                for t in range(TILES):
                    for g in [3 * j + ky for j in far_chunks(t) for ky in range(3)]:
                        if g:
                            pe.wait_ge(fz_lo, ZG * b + g)
                        z_product(g, par).then_inc(fz_ps, 1)
                    for ky in range(3):
                        pe.wait_ge(f_st, 24 * b + 3 * t + ky + 1)
                        for v in far_of(t, ky):
                            f = far_units[v][2]
                            if v >= 2:
                                pe.wait_ge(fs_lo, FAR_UNITS * b + v - 1)
                            for kx in range(3):
                                mm = pe.transpose(sps[v % 2][:, kx * P:(kx + 1) * P],
                                                  sTf[:, kx, f * P:(f + 1) * P], eye32[:, :])
                            mm.then_inc(fs_ps, 1)
                            pe.wait_ge(fs_lo, FAR_UNITS * b + v + 1)
                            start = ky == 0 and v == far_of(t, 0)[0]
                            if start:
                                pe.wait_ge(fz_lo, ZG * b + 3 * min(t + FAR[-1] + 1, CHUNKS))
                                if t:
                                    pe.wait_ge(fy_pm, TILES * b + t)
                            s_product(v, (t + FAR[f]) % Z_RING, ky, start, v == far_of(t, 2)[-1])\
                                .then_inc(fsz_done, 1)
                    pe.wait_ge(fy_pm, TILES * b + t + 1)
                    if t:
                        pe.wait_ge(fy_ch, TILES * b + t)
                    for m in range(2):
                        mm = pe.transpose(yt[:, m * P:(m + 1) * P], ypm[:, t % 4, m * P:(m + 1) * P], eye32[:, :])
                    mm.then_inc(fyt_ps, 1)
                pe.wait_ge(fy_ch, TILES * (b + 1))

            def part1(b, par, more):
                for g in range(6):
                    z_group(g, b, par)
                turn_s(0, b)
                turn_s(1, b)
                for u in range(UNITS):
                    if u % 2 == 0 and u // 2 + 6 < ZG:
                        z_group(u // 2 + 6, b, par)
                    if u + 2 < UNITS:
                        turn_s(u + 2, b)
                    convolve(u, b)
                    if u % 12 == 2 and u > 12:
                        turn_y(u // 12 - 1, b)
                    if more:
                        part0(u, b + 1, 1 - par)
                turn_y(3, b)
                where_far(pe, b, par, far_pass, (fz_ps, ZG), (fs_ps, FAR_UNITS), (fsz_done, FAR_UNITS),
                          (fyt_ps, TILES))

            wq, wk = wqk[:, :, 0:C], wqk[:, :, C:2 * C]
            images((part0, part1), pe)

        @block.scalar
        def _(act):
            act.wait_ge(const_in, CONST_DMAS * 16)
            act.wait_ge(pool_setup, 1)

            def normalize(src, hi_a, hi_b, n, b):
                act.wait_ge(gn_bias, 2 * b + n + 1)
                if n == 0 and not first(b):
                    act.wait_ge(mx_ps, 4 * b)
                if n or not first(b):
                    act.wait_ge(xn_lo, 4 * b + 2 * n)
                for i, hi in ((0, hi_a), (1, hi_b)):
                    act.activation(xn[:, i], src[:, i], ACT.Identity, scale=rstd[:, i:i + 1],
                                   bias=nbias[:, i:i + 1])
                    act.activation(hi, src[:, i], ACT.Identity, scale=rstd[:, i:i + 1],
                                   bias=nbias[:, i:i + 1]).then_inc(xn_hi, 1)

            def copy_blocks(dst, src, n):
                for m in range(2):
                    ins = act.copy(dst[0:ROWS[m], m], src[0:ROWS[m], m * n:(m + 1) * n])
                return ins

            def part0(u, b, par):
                if u == 4:
                    normalize(xin, xh_a[:, :], xhl_b[:, :], 0, b)
                if 8 <= u < 12:
                    r = u - 8
                    act.wait_ge(xt_ps, 4 * b + r + 1)
                    o = l0[r % 2][:, :].bitcast(F16)
                    act.copy(xt[:, 2 * r:2 * r + 2, :], o[:, 0:6 * P].rearrange("p (t n) -> p t n", t=2))\
                       .then_inc(xt_sb, 1)
                if u == 15:
                    act.wait_ge(t1_ps, b + 1)
                    copy_blocks(t1, l0[1], C).then_inc(t1_sb, 1)
                if u == 18:
                    act.wait_ge(log_max, b + 1)
                    for m in range(2):
                        r = ROWS[m]
                        ins = act.activation(prob[0:r, m], l0[0][0:r, m * C:(m + 1) * C], ACT.Exp, scale=HEAD_SCALE,
                                             bias=nmaxs[0:r, m:m + 1], accum_out=rsum[0:r, m:m + 1])
                    ins.then_inc(prob_exp, 1)
                if u == 20:
                    act.wait_ge(r_ps, b + 1)
                    copy_blocks(rmat, l0[1], 2 * P).then_inc(r_sb, 1)
                if u == 22:
                    act.wait_ge(mt_ps, b + 1)
                    act.copy(flat(mt_h), l0[0][:, :]).then_inc(mt_hi, 1)
                if u == 33:
                    inner = lambda t: t[:, par, PAD_T * W:PAD_T * W + N]
                    if not isinstance(b, int) or b >= 2:
                        act.wait_ge(sz_done, UNITS * (b - 1))
                    normalize(x1, inner(x2[0]), inner(x2[2]), 1, b)
                if u == 45:
                    act.wait_ge(off_sb, b + 1)
                    act.activation(mask[:, par], off[:, par, :, 2 * TAPS:J], ACT.Tanh, scale=0.5)
                    act.wait_ge(d_sb, b + 1)
                    act.activation(ay[:, par], ay[:, par], ACT.Abs)
                    act.activation(bx[:, par], bx[:, par], ACT.Abs)
                    act.drain()
                    act.activation(ay[:, par], ay[:, par], ACT.Relu, scale=-1.0, bias=1.0)
                    act.activation(bx[:, par], bx[:, par], ACT.Relu, scale=-1.0, bias=1.0).then_inc(hat_act, 1)

            def split_z(g, b):
                j = g // 3
                if j < Z_RING:
                    if g == 0 and not first(b):
                        act.wait_ge(sz_done, UNITS * b)
                elif g % 3 == 0:
                    act.wait_ge(sz_done, UNITS * b + 6 * (j - Z_RING + 1))
                act.wait_ge(z_ps, ZG * b + g + 1)
                act.copy(zh[:, g // 3 % Z_RING, g % 3].rearrange("p (h n) -> p h n", h=2), zps[:, :, 0:KO // 2])\
                   .then_inc(z_hi, 1)

            def far_pass(b, par):
                act.wait_ge(sz_done, UNITS * (b + 1))
                act.wait_ge(yt_ps, 4 * (b + 1))
                for t in range(TILES):
                    for g in [3 * j + ky for j in far_chunks(t) for ky in range(3)]:
                        if t and g % 3 == 0:
                            act.wait_ge(fsz_done, FAR_UNITS * b + far_end(t - 1))
                        act.wait_ge(fz_ps, ZG * b + g + 1)
                        act.copy(zh[:, g // 3 % Z_RING, g % 3].rearrange("p (h n) -> p h n", h=2),
                                 zps[:, :, 0:KO // 2]).then_inc(fz_hi, 1)
                    for ky in range(3):
                        for v in far_of(t, ky):
                            act.wait_ge(fs_ps, FAR_UNITS * b + v + 1)
                            if v >= S_RING:
                                act.wait_ge(fsz_done, FAR_UNITS * b + v - S_RING + 1)
                            act.copy(sh[:, v % S_RING].rearrange("p k n -> p (k n)"), sps[v % 2][:, 0:3 * P])\
                               .then_inc(fs_hi, 1)
                    act.wait_ge(fsz_done, FAR_UNITS * b + far_end(t))
                    if t >= 4:
                        act.wait_ge(fyt_ps, TILES * b + t - 3)
                    act.copy(ypm[:, t % 4, 0:C], acc[:, 0:C])
                    act.copy(ypm[:, t % 4, C:2 * P], acc[:, P:C]).then_inc(fy_pm, 1)
                act.wait_ge(fyt_ps, TILES * (b + 1))

            def split_s(u, b):
                act.wait_ge(s_ps, UNITS * b + u + 1)
                if u >= S_RING or not first(b):
                    act.wait_ge(sz_done, UNITS * b + u - S_RING + 1)
                act.copy(sh[:, u % S_RING].rearrange("p k n -> p (k n)"), sps[u % 2][:, 0:3 * P]).then_inc(s_hi, 1)

            def part1(b, par, more):
                for g in range(6):
                    split_z(g, b)
                split_s(0, b)
                split_s(1, b)
                for u in range(UNITS):
                    if u % 2 == 0 and u // 2 + 6 < ZG:
                        split_z(u // 2 + 6, b)
                    if u + 2 < UNITS:
                        split_s(u + 2, b)
                    if u % 6 == 5:
                        t = u // 6
                        act.wait_ge(sz_done, UNITS * b + u + 1)
                        if t >= 4 or not first(b):
                            act.wait_ge(yt_ps, 4 * b + t // 2 - 1)
                        act.copy(ypm[:, t % 4, 0:C], acc[:, 0:C])
                        act.copy(ypm[:, t % 4, C:2 * P], acc[:, P:C]).then_inc(y_pm, 1)
                    if more:
                        part0(u, b + 1, 1 - par)
                where_far(act, b, par, far_pass, (fz_hi, ZG), (fs_hi, FAR_UNITS), (fy_pm, TILES))

            images((part0, part1), act)

            act.wait_ge(bn_done, 1)

            def gelu_pair(q, slot):
                act.wait_ge(f_loaded[slot], 64 * (q - slot) + 128)
                for i in range(3):
                    m = i // 2
                    act.activation(fin_y[slot][:, i], fin_y[slot][:, i], ACT.Gelu, scale=ga[:, m:m + 1],
                                   bias=gb[:, m:m + 1]).then_inc(f_gelu, 1)

            with act.Fori(0, NB // 2 - 1, 2) as q:
                gelu_pair(q, 0)
                gelu_pair(q + 1, 1)

        @block.vector
        def _(dve):
            dve.wait_ge(const_in, CONST_DMAS * 16)
            for i, stage in enumerate((off_stage, proj_stage)):
                dve.tensor_reduce(wmaxt[:, i:i + 1], stage, AX.XY, ALU.max, apply_absolute_value=True)
            dve.drain()
            dve.tensor_scalar(wmax[:, :], wmaxt[:, :], 1e-30, 1e30, ALU.max, ALU.min).then_inc(dve_setup, 1)
            dve.tensor_copy(eye16[:, :], eye32[:, :])
            dve.tensor_scalar(cmid[:, :], cy_sb[:, 0:1], -CENTRE, None, ALU.add)
            dve.wait_ge(pe_setup, 1)
            dve.tensor_reduce(wmaxt[:, :], l0[0][:, 0:2 * P].rearrange("p (i n) -> p i n", i=2), AX.X, ALU.max)
            dve.drain()
            dve.tensor_scalar(unscale[:, :].bitcast(I32), wmaxt[:, :].bitcast(I32), 0x7F800000, None,
                              ALU.bitwise_and)
            dve.drain()
            dve.reciprocal(scale[:, :], unscale[:, :])
            dve.drain()
            for i, (stage, w_h, w_l) in enumerate(((off_stage, flat2(wof_h), flat2(wof_l)),
                                                   (proj_stage, flat2(wpr_h), flat2(wpr_l)))):
                dve.tensor_scalar(stage, stage, scale[:, i:i + 1], None, ALU.mult)
                dve.drain()
                dve.tensor_copy(w_h, stage)
                dve.drain()
                ins = dve.tensor_tensor(w_l, stage, w_h, ALU.subtract)
            ins.then_inc(dve_setup, 1)
            dve.wait_ge(dve_setup, 2)

            def channel_stats(src, n, b):
                for i in range(2):
                    for half in range(2):
                        dve.bn_stats(stats[:, i, half], src[:, i, half * 512:half * 512 + 512])
                dve.drain()
                for i in range(2):
                    dve.bn_aggr(mv[:, i], stats[:, i].rearrange("p a b -> p (a b)"))
                dve.drain()
                dve.tensor_tensor(msq[:, :], mv[:, :, 0], mv[:, :, 0], ALU.mult)
                dve.drain()
                dve.tensor_tensor(mv[:, :, 1], mv[:, :, 1], msq[:, :], ALU.add).then_inc(gn_stats, 1)

            def group_variance(n, b):
                dve.wait_ge(gn_group, 2 * b + n + 1)
                if n or not first(b):
                    dve.wait_ge(xn_hi, 4 * b + 2 * n)
                dve.tensor_copy(flat(gmv), l0[0][:, 0:4])
                dve.drain()
                dve.tensor_tensor(msq[:, :], gmv[:, :, 0], gmv[:, :, 0], ALU.mult)
                dve.drain()
                dve.scalar_tensor_tensor(out=gvar[:, :], in0=gmv[:, :, 1], scalar=GN_EPS, in1=msq[:, :],
                                         op0=ALU.add, op1=ALU.subtract).then_inc(gn_var, 1)

            def residue(lo_a, hi_a, hl_b, n, b):
                for i in range(2):
                    dve.wait_ge(xn_hi, 4 * b + 2 * n + i + 1)
                    if i == 0:
                        dve.tensor_tensor(lo_a, xn[:, 0], hi_a, ALU.subtract).then_inc(xn_lo, 1)
                    else:
                        dve.tensor_tensor(hl_b, xn[CB:P, 1], hl_b, ALU.subtract).then_inc(xn_lo, 1)

            def part0(u, b, par):
                if u == 0:
                    dve.wait_ge(x_loaded, 48 * b + 48)
                    channel_stats(xin, 0, b)
                if u == 2:
                    group_variance(0, b)
                if u == 7:
                    residue(xl_a[:, :], xh_a[:, :], xhl_b[CB:P, :], 0, b)
                if u == 13:
                    dve.wait_ge(gram_ps, b + 1)
                    for m in range(2):
                        ins = dve.tensor_copy(gram[0:ROWS[m], m], l0[0][0:ROWS[m], m * C:(m + 1) * C])
                    ins.then_inc(gram_sb, 1)
                if u == 17:
                    dve.wait_ge(log_ps, b + 1)
                    for m in range(2):
                        dve.tensor_reduce(nmax[0:ROWS[m], m:m + 1], l0[0][0:ROWS[m], m * C:(m + 1) * C], AX.X,
                                          ALU.max, negate=True)
                    dve.drain()
                    for m in range(2):
                        r = ROWS[m]
                        ins = dve.tensor_scalar(nmaxs[0:r, m:m + 1], nmax[0:r, m:m + 1], HEAD_SCALE, None, ALU.mult)
                    ins.then_inc(log_max, 1)
                if u == 19:
                    dve.wait_ge(prob_exp, b + 1)
                    for m in range(2):
                        dve.reciprocal(rinv[0:ROWS[m], m:m + 1], rsum[0:ROWS[m], m:m + 1])
                    dve.drain()
                    for m in range(2):
                        r = ROWS[m]
                        ins = dve.tensor_scalar(prob[0:r, m], prob[0:r, m], rinv[0:r, m:m + 1], None, ALU.mult)
                    ins.then_inc(prob_sb, 1)
                if u == 22:
                    dve.wait_ge(mt_hi, b + 1)
                    dve.tensor_tensor(flat(mt_l), l0[0][:, :], flat(mt_h), ALU.subtract).then_inc(mt_lo, 1)
                if 24 <= u < 28:
                    q = u - 24
                    m, n = q // 2, slice(q % 2 * 512, q % 2 * 512 + 512)
                    dve.wait_ge(mx_ps, 4 * b + q + 1)
                    if q == 0 and not first(b):
                        dve.wait_ge(x1_stored, 32 * b)
                    dve.scalar_tensor_tensor(out=x1[:, m, n], in0=l0[(q + 1) % 2][:, :], scalar=bo[:, m:m + 1],
                                             in1=xin[:, m, n], op0=ALU.add, op1=ALU.add).then_inc(x1_sb, 1)
                if u == 29:
                    dve.wait_ge(x1_sb, 4 * b + 4)
                    channel_stats(x1, 1, b)
                if u == 30:
                    group_variance(1, b)
                if u == 35:
                    inner = lambda t: t[:, par, PAD_T * W:PAD_T * W + N]
                    residue(inner(x2[1]), inner(x2[0]), inner(x2[2])[CB:P], 1, b)
                    dve.wait_ge(xn_lo, 4 * b + 4)
                    if not first(b):
                        dve.wait_ge(off_ps, b)
                    for src, dst in zip(x2, x2s):
                        rows = lambda t, i: t[:, i, PAD_T * W:PAD_T * W + N].rearrange("p (h w) -> p h w", h=H)
                        dve.tensor_copy(rows(dst, 0)[:, :, 1:W], rows(src, par)[:, :, 0:W - 1])
                        ins = dve.tensor_copy(rows(dst, 1)[:, :, 0:W - 1], rows(src, par)[:, :, 1:W])
                    ins.then_inc(x2_moved, 1)
                if u == 44:
                    dve.wait_ge(off_ps, b + 1)
                    if not isinstance(b, int) or b >= 2:
                        dve.wait_ge(st_made, 24 * (b - 1))
                    dve.scalar_tensor_tensor(out=flat(off[:, par]), in0=l0[1][:, 0:TILES * J],
                                             scalar=unscale[:, 0:1], in1=flat(boff), op0=ALU.mult, op1=ALU.add)
                    dve.drain()
                    yx = off[:, par, :, 0:2 * TAPS]
                    dve.tensor_scalar(yx, yx, -MAX_OFF, MAX_OFF, ALU.max, ALU.min).then_inc(off_sb, 1)
                    dve.wait_ge(off_sb, b + 1)
                    dve.tensor_tensor(hat4(ay, par, R), spread(off[:, par, :, 0:TAPS], R),
                                      cy_sb[:, None, None, 0:R].broadcast_to([P, TILES, TAPS, R]), ALU.add)
                    dve.tensor_tensor(hat4(bx, par, W), spread(off[:, par, :, TAPS:2 * TAPS], W),
                                      cx_sb[:, None, :, :].broadcast_to([P, TILES, TAPS, W]), ALU.add)\
                       .then_inc(d_sb, 1)
                    dve.tensor_scalar(ypos[:, :, :], off[:, par, :, 0:TAPS], cmid[:, 0:1], None, ALU.add)
                    dve.drain()
                    dve.tensor_reduce(offmax[:, :], ypos[:, :, :], AX.XY, ALU.max,
                                      apply_absolute_value=True).then_inc(omax_sb, 1)
                if u == 46:
                    dve.wait_ge(hat_act, b + 1)
                    dve.tensor_scalar(mask[:, par], mask[:, par], 1.0, None, ALU.add)
                    dve.drain()
                    dve.tensor_tensor(hat4(ay, par, R), hat4(ay, par, R), spread(mask[:, par], R), ALU.mult)\
                       .then_inc(hats, 1)
                if u == 47:
                    dve.wait_ge(omax_ps, b + 1)
                    dve.tensor_reduce(offmaxg[:, :], l0[0][:, 0:P], AX.X, ALU.max)
                    dve.drain()
                    dve.tensor_scalar(far[:, par:par + 1], offmaxg[:, :], CENTRE, None, ALU.is_gt).then_inc(flag_sb, 1)

            def split_z(g, b):
                dve.wait_ge(z_hi, ZG * b + g + 1)
                half = lambda t: t[:, g // 3 % Z_RING, g % 3].rearrange("p (h n) -> p h n", h=2)
                dve.tensor_tensor(half(zl), zps[:, :, 0:KO // 2], half(zh), ALU.subtract).then_inc(z_lo, 1)

            def split_s(u, b):
                dve.wait_ge(s_hi, UNITS * b + u + 1)
                one = lambda t: t[:, u % S_RING].rearrange("p k n -> p (k n)")
                dve.tensor_tensor(one(sl), sps[u % 2][:, 0:3 * P], one(sh), ALU.subtract).then_inc(s_lo, 1)

            def far_pass(b, par):
                rows4 = ayf.rearrange("p (t k) r -> p t k r", t=TILES)
                dve.tensor_tensor(rows4, spread(off[:, par, :, 0:TAPS], FAR_ROWS),
                                  cy_sb[:, None, None, R:R + FAR_ROWS].broadcast_to([P, TILES, TAPS, FAR_ROWS]),
                                  ALU.add)
                dve.drain()
                dve.scalar_tensor_tensor(out=ayf, in0=ayf, scalar=-1.0, in1=ayf, op0=ALU.mult, op1=ALU.min)
                dve.drain()
                dve.tensor_scalar(ayf, ayf, 1.0, 0.0, ALU.add, ALU.max)
                dve.drain()
                dve.tensor_tensor(rows4, rows4, spread(mask[:, par], FAR_ROWS), ALU.mult)
                dve.drain()
                for t in range(TILES):
                    for g in [3 * j + ky for j in far_chunks(t) for ky in range(3)]:
                        dve.wait_ge(fz_hi, ZG * b + g + 1)
                        half = lambda v: v[:, g // 3 % Z_RING, g % 3].rearrange("p (h n) -> p h n", h=2)
                        dve.tensor_tensor(half(zl), zps[:, :, 0:KO // 2], half(zh), ALU.subtract).then_inc(fz_lo, 1)
                    for ky in range(3):
                        v0 = far_of(t, ky)[0]
                        if v0:
                            dve.wait_ge(fs_ps, FAR_UNITS * b + v0)
                        k = t * TAPS + 3 * ky
                        for kx in range(3):
                            ins = dve.tensor_tensor(
                                sTf[:, kx].rearrange("p (r x) -> p r x", r=FAR_ROWS),
                                ayf[:, k + kx, :, None].broadcast_to([P, FAR_ROWS, W]),
                                bx[:, par, k + kx, None, :].broadcast_to([P, FAR_ROWS, W]), ALU.mult)
                        ins.then_inc(f_st, 1)
                        for v in far_of(t, ky):
                            dve.wait_ge(fs_hi, FAR_UNITS * b + v + 1)
                            one = lambda w: w[:, v % S_RING].rearrange("p k n -> p (k n)")
                            dve.tensor_tensor(one(sl), sps[v % 2][:, 0:3 * P], one(sh), ALU.subtract)\
                               .then_inc(fs_lo, 1)
                    dve.wait_ge(fyt_ps, TILES * b + t + 1)
                    for m in range(2):
                        y = ych[:, par, m, t * P:(t + 1) * P]
                        ins = dve.scalar_tensor_tensor(out=y, in0=yt[:, m * P:(m + 1) * P], scalar=unscale[:, 1:2],
                                                       in1=y, op0=ALU.mult, op1=ALU.add)
                    ins.then_inc(fy_ch, 1)

            def scale_y(q, b, par):
                dve.wait_ge(yt_ps, 4 * b + q + 1)
                if q == 0:
                    dve.wait_ge(y_free[par], 32 + 16 * (b - par))
                for m in range(2):
                    ins = dve.tensor_scalar(ych[:, par, m, q * 2 * P:(q + 1) * 2 * P], yt[:, m * 2 * P:(m + 1) * 2 * P],
                                            unscale[:, 1:2], pb[:, m:m + 1], ALU.mult, ALU.add)
                ins.then_inc(y_ch, 1)

            def part1(b, par, more):
                for g in range(6):
                    split_z(g, b)
                split_s(0, b)
                split_s(1, b)
                for u in range(UNITS):
                    if u % 2 == 0 and u // 2 + 6 < ZG:
                        split_z(u // 2 + 6, b)
                    if u + 2 < UNITS:
                        split_s(u + 2, b)
                    if u % 12 == 3 and u > 12:
                        scale_y(u // 12 - 1, b, par)
                    if more:
                        part0(u, b + 1, 1 - par)
                scale_y(3, b, par)
                where_far(dve, b, par, far_pass, (fz_lo, ZG), (f_st, 3 * TILES), (fs_lo, FAR_UNITS), (fy_ch, TILES))
                dve.drain()
                for m in range(2):
                    for half in range(2):
                        ins = dve.bn_stats(ystats[:, m, bass.ds(2 * b + half, 1), :],
                                           ych[:, par, m, half * 512:(half + 1) * 512])
                ins.then_inc(y_final, 1)

            images((part0, part1), dve)

            dve.wait_ge(y_final, NB)
            for m in range(2):
                dve.bn_aggr(ymv[:, m], ystats[:, m].rearrange("p a b -> p (a b)"))
            dve.drain()
            dve.tensor_scalar(yvar[:, :], ymv[:, :, 1], BN_EPS, None, ALU.add).then_inc(bn_var, 1)
            dve.wait_ge(bn_rstd, 1)
            dve.tensor_tensor(ga[:, :], gam[:, :], yrstd[:, :], ALU.mult)
            dve.drain()
            dve.tensor_tensor(gmean[:, :], ymv[:, :, 0], ga[:, :], ALU.mult)
            dve.drain()
            dve.tensor_tensor(gb[:, :], bet[:, :], gmean[:, :], ALU.subtract).then_inc(bn_done, 1)

            def add_pair(q, slot):
                for i in range(3):
                    dve.wait_ge(f_gelu, 3 * q + i + 1)
                    dve.tensor_tensor(fin_y[slot][:, i], fin_y[slot][:, i], fin_x[slot][:, i], ALU.add)\
                       .then_inc(f_sum, 1)

            with dve.Fori(0, NB // 2 - 1, 2) as q:
                add_pair(q, 0)
                add_pair(q + 1, 1)

        @block.gpsimd
        def _(pool):
            pool.memset(mhalf[:, :], -0.5)
            pool.memset(minus[:, :], -1.0)
            for t in (*x2, *x2s):
                ins = pool.memset(t[:, :, :], 0.0)
            ins.then_inc(pool_setup, 1)
            pool.wait_ge(pool_setup, 1)
            pool.wait_ge(const_in, CONST_DMAS * 16)

            def group_rstd(n, b):
                pool.wait_ge(gn_var, 2 * b + n + 1)
                pool.tensor_tensor(rstd[:, :], gvar[:, :], mhalf[:, :], ALU.pow).then_inc(gn_rstd, 1)
                pool.wait_ge(gn_rstd, 2 * b + n + 1)
                pool.tensor_tensor(nbias[:, :], gmv[:, :, 0], rstd[:, :], ALU.mult).then_inc(gn_mean, 1)
                pool.wait_ge(gn_mean, 2 * b + n + 1)
                pool.tensor_tensor(nbias[:, :], nbias[:, :], minus[:, :], ALU.mult).then_inc(gn_bias, 1)

            def part0(u, b, par):
                if u == 3:
                    group_rstd(0, b)
                if u == 31:
                    group_rstd(1, b)

            def part1(b, par, more):
                for p in range(3 * TILES):
                    t, ky = divmod(p, 3)
                    if p == 0:
                        pool.wait_ge(hats, b + 1)
                    if p >= ST_RING or not first(b):
                        pool.wait_ge(s_ps, UNITS * b + 2 * (p - ST_RING) + 2)
                    k = t * TAPS + 3 * ky
                    a = ay[:, par, k:k + 3, :, None].broadcast_to([P, 3, R, W])
                    x_ = bx[:, par, k:k + 3, None, :].broadcast_to([P, 3, R, W])
                    pool.tensor_tensor(sT[:, p % ST_RING].rearrange("p k (r x) -> p k r x", r=R), a, x_, ALU.mult)\
                        .then_inc(st_made, 1)
                    if more:
                        for u in (2 * p - 4, 2 * p - 3):
                            part0(u, b + 1, 1 - par)

            images((part0, part1), pool)

            pool.wait_ge(bn_var, 1)
            pool.tensor_tensor(yrstd[:, :], yvar[:, :], mhalf[:, :], ALU.pow).then_inc(bn_rstd, 1)

            def store_pair(q, slot):
                pool.wait_ge(f_sum, 3 * q + 3)
                for i in range(2):
                    pool.dma_start(out[2 * q + i, 0:P], fin_y[slot][:, i]).then_inc(f_stored[slot], 16)
                    pool.dma_start(out[2 * q + i, P:C], fin_y[slot][CB * i:CB * i + CB, 2]).then_inc(f_stored[slot], 16)

            with pool.Fori(0, NB // 2 - 1, 2) as q:
                store_pair(q, 0)
                store_pair(q + 1, 1)
            for i in range(2):
                pool.wait_ge(f_stored[i], 16 * NB)

    return nc


def kernel(x, L0_conv_w_qkv, L0_conv_w_out, L0_conv_b_out, L1_conv_proj_w, L1_conv_proj_b, L1_conv_off_w,
           L1_conv_off_b, L1_conv_mask_w, L1_conv_mask_b, L1_conv_gamma, L1_conv_beta):
    import concourse.bacc as bacc
    from concourse.bass_utils import run_bass_kernel_spmd as run

    x = np.asarray(x)
    nb = x.shape[0]
    w_qkv = np.asarray(L0_conv_w_qkv)
    w_off = np.asarray(L1_conv_off_w)
    taps_last = lambda w: np.transpose(w, (1, 2, 3, 0))
    w_27 = np.concatenate([w_off[0::2], w_off[1::2], np.asarray(L1_conv_mask_w)], axis=0)
    b_off = np.asarray(L1_conv_off_b)
    b_27 = np.concatenate([b_off[0::2], b_off[1::2], np.asarray(L1_conv_mask_b)], axis=0)
    avg, cy, cx, eye = coordinate_tables()
    arrays = {
        "x": x.reshape(nb, C, N),
        "w_qkT": w_qkv[0:2 * C].T,
        "w_v": w_qkv[2 * C:3 * C],
        "w_outT": np.asarray(L0_conv_w_out).T,
        "b_out": np.asarray(L0_conv_b_out),
        "w_off": taps_last(w_27).reshape(C, TAPS * J),
        "b_off": b_27,
        "w_proj": taps_last(np.asarray(L1_conv_proj_w)).reshape(C, TAPS * C),
        "proj_b": np.asarray(L1_conv_proj_b),
        "gamma": np.asarray(L1_conv_gamma),
        "beta": np.asarray(L1_conv_beta),
        "avg": avg, "cy": cy, "cx": cx, "eye": eye,
    }
    nc = bacc.Bacc("TRN2", target_bir_lowering=False, num_devices=1)
    arrays = {f"in_{k}": np.ascontiguousarray(v) for k, v in arrays.items()}
    args = [nc.dram_tensor(k, v.shape, mybir.dt.from_np(v.dtype), kind="ExternalInput").ap()
            for k, v in arrays.items()]
    args.append(nc.dram_tensor("out", (nb, C, N), F32, kind="ExternalOutput").ap())
    build(nc, *args)
    r = run(nc, [arrays], core_ids=[0])
    return r.results[0]["out"].reshape(nb, C, H, W)
```

```python
from contextlib import ExitStack

import numpy as np
import concourse.bass as bass
from concourse import mybir

F32, F16, I32 = mybir.dt.float32, mybir.dt.float16, mybir.dt.int32
ALU = mybir.AluOpType
ACT = mybir.ActivationFunctionType
AX = mybir.AxisListType

P = 128
C, H, W = 192, 32, 32
N = H * W
CB = C - P
TAPS = 9
J = 3 * TAPS
GROUPS = 32
ROWS_T = P // W
TILES = N // P
CHUNKS = TILES
R = 2 * ROWS_T
CENTRE = (R - 1) / 2
MAX_OFF = float(min(H, W) // 4)
PAD_T, PAD_ROWS = 1, H + 2
WRAP = 3
KO = 3 * C
UNITS = 6 * TILES
HEAD_SCALE = float((C // 4) ** (-0.5))
GN_EPS = 1e-5
BN_EPS = 1e-5
FAR = [-2, -1, 2, 3]
NEAR_ROWS = list(range(R))
FAR_ROWS = [ROWS_T * f + r for f in FAR for r in range(ROWS_T)]


def outside(t, ky, rows):
    at = [ROWS_T * t + ky - 3 + r for r in rows]
    return sum(r < 0 for r in at), sum(r >= H for r in at)


def coordinate_tables():
    c = np.concatenate([np.arange(P), np.arange(P, C), np.arange(P, C)])
    g = c // (C // GROUPS)
    avg = np.zeros((P, 4, P), np.float32)
    for fb in range(2):
        for tb in range(2):
            same = g[fb * P:fb * P + P, None] == g[None, tb * P:tb * P + P]
            avg[:, 2 * fb + tb, :] = same * np.float32(1.0 / (C // GROUPS))
    p = np.arange(P)
    cy = (p[:, None] // W + 2 - np.array(NEAR_ROWS + FAR_ROWS)[None, :]).astype(np.float32)
    k = np.arange(TAPS)
    cx = (p[:, None, None] % W - 1 + (k % 3)[None, :, None] - np.arange(W)[None, None, :]).astype(np.float32)
    return avg.reshape(P, -1), cy, cx.reshape(P, -1), np.eye(P, dtype=np.float32)


def build(nc, x, w_qkT, w_v, w_outT, b_out, w_off, b_off, w_proj, proj_b, gamma, beta,
          avg, cy, cx, eye, out):
    NB = x.shape[0]
    nc.disable_value_cache = True
    x1_dram = nc.dram_tensor("x1_scratch", [NB, C, N], F32, kind="Internal").ap()
    y_dram = nc.dram_tensor("y_scratch", [NB, C, N], F32, kind="Internal").ap()

    with ExitStack() as ctx:
        def sb(name, shape, dt=F32):
            return ctx.enter_context(nc.sbuf_tensor(name, shape, dt))

        def bank(name, shape=(P, 512), dt=F32):
            return ctx.enter_context(nc.psum_tensor(name, list(shape), dt))

        def sem(name):
            return ctx.enter_context(nc.semaphore(name))

        avg_sb = sb("avg_sb", [P, 4, P])
        cy_sb = sb("cy_sb", [P, R + len(FAR_ROWS)])
        cx_sb = sb("cx_sb", [P, TAPS, W])
        eye32 = sb("eye32", [P, P])
        eye16 = sb("eye16", [P, P], F16)
        mhalf = sb("mhalf", [P, 2])
        minus = sb("minus", [P, 2])
        wqk = sb("wqk", [P, 2, 2 * C])
        wv = sb("wv", [P, 2, 2 * P])
        wo = sb("wo", [P, 2, C])
        wof = sb("wof", [P, 2, TAPS, 2, J], F16)
        wpr_h = sb("wpr_h", [P, 2, 3, KO], F16)
        wpr_l = sb("wpr_l", [P, 2, 3, KO], F16)
        bo = sb("bo", [P, 2])
        pb = sb("pb", [P, 2])
        gam = sb("gam", [P, 2])
        bet = sb("bet", [P, 2])
        boff = sb("boff", [P, TILES, J])
        wmax = sb("wmax", [P, 2])
        wmaxt = sb("wmaxt", [P, 2])
        unscale = sb("unscale", [P, 2])
        scale = sb("scale", [P, 2])
        xin = sb("xin", [P, 2, N])
        xn = sb("xn", [P, 2, N])
        x1 = sb("x1", [P, 2, N])
        stats = sb("stats", [P, 2, 2, 6])
        mv = sb("mv", [P, 2, 2])
        msq = sb("msq", [P, 2])
        gmv = sb("gmv", [P, 2, 2])
        gvar = sb("gvar", [P, 2])
        rstd = sb("rstd", [P, 2])
        nbias = sb("nbias", [P, 2])
        xh_a = sb("xh_a", [P, N], F16)
        xl_a = sb("xl_a", [P, N], F16)
        xhl_b = sb("xhl_b", [P, N], F16)
        xt = sb("xt", [P, TILES, 2 * C], F16)
        gram = sb("gram", [P, 2, C])
        prob = gram
        t1 = sb("t1", [P, 2, C])
        rmat = sb("rmat", [P, 2, C])
        mt_h = sb("mt_h", [P, 2, 2 * P], F16)
        mt_l = sb("mt_l", [P, 2, 2 * P], F16)
        nmax = sb("nmax", [P, 2])
        nmaxs = sb("nmaxs", [P, 2])
        rsum = sb("rsum", [P, 2])
        rinv = sb("rinv", [P, 2])
        x2s = [sb(f"x2s_{n}", [P, 2, PAD_ROWS * W], F16) for n in ("hi_a", "lo_a", "hilo_b")]
        x2w = [sb(f"x2w_{n}", [P, 2, 2 * WRAP * W], F16) for n in ("hi_a", "lo_a", "hilo_b")]
        x2 = [sb(f"x2_{n}", [P, 2, PAD_ROWS * W], F16) for n in ("hi_a", "lo_a", "hilo_b")]
        off = sb("off", [P, 2, TILES, J])
        ay = sb("ay", [P, 2, TILES * TAPS, R])
        bx = sb("bx", [P, 2, TILES * TAPS, W])
        mask = sb("mask", [P, 2, TILES, TAPS])
        cmid = sb("cmid", [P, 1])
        ypos = sb("ypos", [P, TILES, TAPS])
        offmax = sb("offmax", [P, 1])
        offmaxg = sb("offmaxg", [P, 1])
        far = sb("far", [P, 2], I32)
        zh = sb("zh", [P, CHUNKS, 3, KO], F16)
        zl = sb("zl", [P, CHUNKS, 3, KO], F16)
        ST_RING = 3
        sT = sb("sT", [P, ST_RING, 3, R * W])
        S_RING = 3
        sh = sb("sh", [P, S_RING, 3, P], F16)
        sl = sb("sl", [P, S_RING, 3, P], F16)
        ypm = sb("ypm", [P, 4, 2 * P])
        ych = sb("ych", [P, 2, N])
        ystats = sb("ystats", [P, 2, NB * 2, 6])
        ymv = sb("ymv", [P, 2, 2])
        yvar = sb("yvar", [P, 2])
        yrstd = sb("yrstd", [P, 2])
        ga = sb("ga", [P, 2])
        gmean = sb("gmean", [P, 2])
        gb = sb("gb", [P, 2])

        acc = bank("acc")
        yt = bank("yt")
        zps = bank("zps", (P, 2, 512))
        sps = [bank(f"sps{i}") for i in range(2)]
        l0 = [bank(f"l0_{i}") for i in range(2)]

        const_in = sem("const_in")
        weights_in = sem("weights_in")
        dve_setup = sem("dve_setup")
        pool_setup = sem("pool_setup")
        pe_setup = sem("pe_setup")
        act_setup = sem("act_setup")
        x_loaded = sem("x_loaded")
        gn_stats = sem("gn_stats")
        gn_group = sem("gn_group")
        gn_var = sem("gn_var")
        gn_rstd = sem("gn_rstd")
        gn_mean = sem("gn_mean")
        gn_bias = sem("gn_bias")
        xn_hi = sem("xn_hi")
        xn_lo = sem("xn_lo")
        xt_ps = sem("xt_ps")
        xt_sb = sem("xt_sb")
        gram_ps = sem("gram_ps")
        gram_sb = sem("gram_sb")
        t1_ps = sem("t1_ps")
        t1_sb = sem("t1_sb")
        log_ps = sem("log_ps")
        log_max = sem("log_max")
        prob_exp = sem("prob_exp")
        prob_sb = sem("prob_sb")
        r_ps = sem("r_ps")
        r_sb = sem("r_sb")
        mt_ps = sem("mt_ps")
        mt_hi = sem("mt_hi")
        mt_lo = sem("mt_lo")
        mx_ps = sem("mx_ps")
        x1_sb = sem("x1_sb")
        x1_stored = sem("x1_stored")
        x2_moved = sem("x2_moved")
        off_ps = sem("off_ps")
        off_sb = sem("off_sb")
        d_sb = sem("d_sb")
        hat_act = sem("hat_act")
        bx_made = sem("bx_made")
        hats = sem("hats")
        omax_sb = sem("omax_sb")
        omax_ps = sem("omax_ps")
        flag_sb = sem("flag_sb")
        z_ps = sem("z_ps")
        z_hi = sem("z_hi")
        z_lo = sem("z_lo")
        st_made = sem("st_made")
        s_ps = sem("s_ps")
        s_hi = sem("s_hi")
        s_lo = sem("s_lo")
        sz_done = sem("sz_done")
        y_pm = sem("y_pm")
        yt_ps = sem("yt_ps")
        y_ch = sem("y_ch")
        y_final = sem("y_final")
        y_stored = sem("y_stored")
        fz_ps = sem("fz_ps")
        fz_hi = sem("fz_hi")
        fz_lo = sem("fz_lo")
        f_st = sem("f_st")
        fs_ps = sem("fs_ps")
        fs_hi = sem("fs_hi")
        fs_lo = sem("fs_lo")
        fsz_done = sem("fsz_done")
        fy_pm = sem("fy_pm")
        fyt_ps = sem("fyt_ps")
        fy_ch = sem("fy_ch")
        flag_seen = sem("flag_seen")
        far_left = sem("far_left")
        bn_var = sem("bn_var")
        bn_rstd = sem("bn_rstd")
        bn_done = sem("bn_done")
        f_loaded = [sem(f"f_loaded{i}") for i in range(2)]
        f_gelu = sem("f_gelu")
        f_sum = sem("f_sum")
        f_stored = [sem(f"f_stored{i}") for i in range(2)]

        ZG = 3 * CHUNKS
        SLOTS = UNITS
        CONST_DMAS = 4 + TILES + 3 + 3 + 4 + 3 * 4

        def flat(t):
            v = t[tuple([slice(None)] * len(t.shape))]
            return v.rearrange("p a b -> p (a b)")

        def flat2(t):
            v = t[:, :, :, :]
            return v.rearrange("p i a b -> p i (a b)")

        def inner(t, par):
            return t[:, par, PAD_T * W:PAD_T * W + N]

        def hat4(t, par, n):
            return t[:, par].rearrange("p (t k) n -> p t k n", t=TILES)

        def spread(v, n):
            return v[:, :, :, None].broadcast_to([P, TILES, TAPS, n])

        zl_flat = zl[:, :, :, :].rearrange("p j k o -> p (j k o)")
        zh_flat = zh[:, :, :, :].rearrange("p j k o -> p (j k o)")
        proj_stage = zl_flat[:, 0:2 * 2 * TAPS * C].bitcast(F32).rearrange("p (i n) -> p i n", i=2)
        off_stage = zh_flat[:, 0:2 * 2 * TAPS * J].bitcast(F32).rearrange("p (i n) -> p i n", i=2)
        ayf = xn[:, :, :].rearrange("p a n -> p (a n)")[:, 0:TILES * TAPS * len(FAR_ROWS)]\
            .rearrange("p (k r) -> p k r", r=len(FAR_ROWS))
        sTf = xt[:, :, :].rearrange("p t n -> p (t n)").bitcast(F32).rearrange("p (k m) -> p k m", k=3)
        in_slots = lambda v: v[:, 0:2 * 2 * 3 * N].bitcast(F32).rearrange("p (s i n) -> p s i n", s=2, i=3)
        fin_y, fin_x = in_slots(zh_flat), in_slots(zl_flat)

        def images(program, eng):
            part0, part1, prepare = program
            for u in range(SLOTS):
                part0(u, 0, 0)
                if u == 15:
                    prepare()
            part1(0, 0, True)
            with eng.Fori(1, NB - 2, 2) as b:
                part1(b, 1, True)
                part1(b + 1, 0, True)
            part1(NB - 1, (NB - 1) % 2, False)

        far_units = [(t, ky, f) for t in range(TILES) for ky in range(3)
                     for f, c in enumerate(FAR) if 0 <= t + c <= CHUNKS]
        FAR_UNITS = len(far_units)
        far_of = lambda t, ky: [v for v, w in enumerate(far_units) if w[0:2] == (t, ky)]
        far_end = lambda t: sum(w[0] <= t for w in far_units)
        AHEAD = 6
        FAR_Z = 2 * AHEAD

        def tile_at(i, par):
            return (i + par * TILES // 2) % TILES

        def last_use(m):
            was = (m + TILES // 2) % TILES
            return was if was else TILES - 1

        def first(b):
            return isinstance(b, int) and b == 0

        ROWS = (P, CB)
        COLS = (slice(0, P), slice(P, C))

        def where_far(eng, b, par, more, far_pass, *counts):
            eng.wait_ge(flag_sb, b + 1)
            eng.sem_inc(flag_seen, 1)
            flag = eng.value_load(far[0:1, par:par + 1], min_val=0, max_val=1)
            with eng.If(flag == 1):
                far_pass(b, par, more)
                eng.sem_inc(far_left, 1)
            with eng.Else():
                for s, n in counts:
                    eng.sem_inc(s, n)

        block = ctx.enter_context(nc.Block())

        @block.sync
        def _(sp):
            def load_blocks(dst, src, done=const_in):
                sp.dma_start(dst[:, 0], src[0:P]).then_inc(done, 16)
                sp.dma_start(dst[0:CB, 1], src[P:C]).then_inc(done, 16)
                sp.dma_start(dst[CB:P, 1], src[P:C]).then_inc(done, 16)

            def load_x(b):
                for dst, src in ((xin[:, 0], x[b, 0:P]), (xin[0:CB, 1], x[b, P:C]), (xin[CB:P, 1], x[b, P:C])):
                    sp.dma_start(dst, src).then_inc(x_loaded, 16)

            load_x(0)
            sp.dma_start(avg_sb[:, :, :], avg.rearrange("p (a b) -> p a b", a=4)).then_inc(const_in, 16)
            sp.dma_start(cy_sb[:, :], cy).then_inc(const_in, 16)
            sp.dma_start(cx_sb[:, :, :], cx.rearrange("p (k x) -> p k x", k=TAPS)).then_inc(const_in, 16)
            sp.dma_start(eye32[:, :], eye).then_inc(const_in, 16)
            for t in range(TILES):
                sp.dma_start(boff[:, t, :], b_off.partition_broadcast(P)).then_inc(const_in, 16)
            load_blocks(wqk, w_qkT)
            load_blocks(wo, w_outT)
            for i in range(2):
                rows = slice(i * P, i * P + ROWS[i])
                sp.dma_start(wv[0:ROWS[i], i, 0:C], w_v[rows]).then_inc(const_in, 16)
                sp.dma_start(wv[0:ROWS[i], i, C:2 * P], w_v[rows, P:C]).then_inc(const_in, 16)
            for dst, src in ((bo, b_out), (pb, proj_b), (gam, gamma), (bet, beta)):
                load_blocks(dst[:, :, None], src[:, None])
            load_blocks(off_stage, w_off, weights_in)
            load_blocks(proj_stage, w_proj, weights_in)

            def attended(b, more=True):
                sp.wait_ge(x1_sb, 4 * b + 4)
                sp.dma_start(x1_dram[b, 0:P], x1[:, 0]).then_inc(x1_stored, 16)
                sp.dma_start(x1_dram[b, P:C], x1[0:CB, 1]).then_inc(x1_stored, 16)
                if more:
                    load_x(b + 1)

            def convolved(b):
                sp.wait_ge(y_final, b + 1)
                sp.dma_start(y_dram[b, 0:P], ych[:, 0]).then_inc(y_stored, 16)
                sp.dma_start(y_dram[b, P:C], ych[0:CB, 1]).then_inc(y_stored, 16)

            attended(0)
            with sp.Fori(1, NB - 2, 2) as b:
                attended(b)
                convolved(b - 1)
                attended(b + 1)
                convolved(b)
            attended(NB - 1, False)
            convolved(NB - 2)
            convolved(NB - 1)

            sp.wait_ge(x1_stored, 32 * NB)
            sp.wait_ge(y_stored, 32 * NB)

            def load_pair(q, slot):
                for dst, src in ((fin_y, y_dram), (fin_x, x1_dram)):
                    for i in range(2):
                        sp.dma_start(dst[:, slot, i], src[2 * q + i, 0:P]).then_inc(f_loaded[slot], 16)
                        sp.dma_start(dst[CB * i:CB * i + CB, slot, 2], src[2 * q + i, P:C]).then_inc(f_loaded[slot], 16)

            sp.wait_ge(bn_var, 1)
            for q in range(2):
                load_pair(q, q)
            with sp.Fori(2, NB // 2 - 1, 2) as q:
                for i in range(2):
                    sp.wait_ge(f_stored[i], 32 * q)
                    load_pair(q + i, i)

        @block.tensor
        def _(pe):
            pe.wait_ge(const_in, CONST_DMAS * 16)
            pe.wait_ge(dve_setup, 1)
            pe.wait_ge(pool_setup, 1)

            def prepare():
                pe.wait_ge(dve_setup, 2)
                for i in range(2):
                    mm = pe.transpose(yt[:, i * P:(i + 1) * P], wmax[:, i:i + 1].broadcast_to([P, P]), eye32[:, :])
                mm.then_inc(pe_setup, 1)
                pe.wait_ge(dve_setup, 3)

            def group_stats(n, b):
                pe.wait_ge(gn_stats, 2 * b + n + 1)
                for tb in range(2):
                    o = l0[0][:, 2 * tb:2 * tb + 2]
                    pe.matmul(o, avg_sb[:, tb, :], mv[:, 0, :], start=True, stop=False)
                    mm = pe.matmul(o, avg_sb[0:CB, 2 + tb, :], mv[0:CB, 1, :], start=False, stop=True)
                mm.then_inc(gn_group, 1)

            def square(done, lhs, rhs, ps, n):
                for m in range(2):
                    o = ps[0:ROWS[m], m * n:(m + 1) * n]
                    pe.matmul(o, lhs[:, 0, COLS[m]], rhs[:, 0], start=True, stop=False)
                    mm = pe.matmul(o, lhs[0:CB, 1, COLS[m]], rhs[0:CB, 1], start=False, stop=True)
                mm.then_inc(done, 1)

            def transpose_x(r, b):
                if r == 0:
                    pe.wait_ge(xn_lo, 4 * b + 2)
                if r >= 2:
                    pe.wait_ge(xt_sb, 4 * b + r - 1)
                o = l0[r % 2][:, :].bitcast(F16)
                for i in range(2):
                    n = slice((2 * r + i) * P, (2 * r + i + 1) * P)
                    for k, src in enumerate((xh_a, xhl_b, xl_a)):
                        mm = pe.transpose(o[:, i * 3 * P + k * P:i * 3 * P + (k + 1) * P], src[:, n], eye16[:, :])
                mm.then_inc(xt_ps, 1)

            def gram_product(m, b):
                pe.wait_ge(xt_sb, 4 * b + 4)
                for t in range(TILES):
                    hi, lo_b, lo_a = xt[:, t, 0:C], xt[:, t, C:2 * P], xt[:, t, 2 * P:3 * P]
                    o = l0[0][0:ROWS[m], m * C:(m + 1) * C]
                    h_m = hi[:, COLS[m]]
                    l_m = (lo_a, lo_b)[m]
                    pe.matmul(o, h_m, hi, start=(t == 0), stop=False)
                    pe.matmul(o[:, 0:P], h_m, lo_a, start=False, stop=False)
                    pe.matmul(o[:, P:C], h_m, lo_b, start=False, stop=False)
                    mm = pe.matmul(o, l_m, hi, start=False, stop=(t == TILES - 1))
                if m == 1:
                    mm.then_inc(gram_ps, 1)

            def apply_m(q, b):
                m, half = divmod(q, 2)
                if q == 0:
                    pe.wait_ge(mt_lo, b + 1)
                if q >= 2:
                    pe.wait_ge(x1_sb, 4 * b + q - 1)
                o = l0[(q + 1) % 2][:, :]
                n = slice(half * 512, half * 512 + 512)
                pe.matmul(o, mt_h[:, 0, m * P:(m + 1) * P], xh_a[:, n], start=True, stop=False)
                pe.matmul(o, mt_h[:, 0, m * P:(m + 1) * P], xl_a[:, n], start=False, stop=False)
                pe.matmul(o, mt_l[:, 0, m * P:(m + 1) * P], xh_a[:, n], start=False, stop=False)
                pe.matmul(o, mt_h[:, 1, m * P:(m + 1) * P], xhl_b[:, n], start=False, stop=False)
                pe.matmul(o, mt_l[:, 1, m * P:(m + 1) * P], xhl_b[:, n], start=False, stop=True).then_inc(mx_ps, 1)

            def offset_conv(t, b, par):
                if t == 0:
                    pe.wait_ge(x2_moved, b + 1)
                o = l0[1][:, t * 2 * J:(t + 1) * 2 * J]
                for k in range(TAPS):
                    row = ROWS_T * t + k // 3 - 1 + PAD_T
                    for n, (plane, m) in enumerate(((0, 0), (1, 0), (2, 1))):
                        src = x2[plane][:, par] if k % 3 == 1 else x2s[plane][:, k % 3 // 2]
                        mm = pe.matmul(o, src[:, row * W:(row + ROWS_T) * W],
                                       wof[:, m, k].rearrange("p i j -> p (i j)"),
                                       start=(k == 0 and n == 0), stop=(k == TAPS - 1 and n == 2))
                if t == TILES - 1:
                    mm.then_inc(off_ps, 1)

            def offset_max(b):
                pe.wait_ge(omax_sb, b + 1)
                pe.transpose(l0[0][:, 0:P], offmax[:, :].broadcast_to([P, P]), eye32[:, :]).then_inc(omax_ps, 1)

            def part0(u, b, par):
                if u == 3:
                    group_stats(0, b)
                if 10 <= u < 14:
                    transpose_x(u - 10, b)
                if 14 <= u < 16:
                    gram_product(u - 14, b)
                if u == 17:
                    pe.wait_ge(gram_sb, b + 1)
                    square(t1_ps, gram, wq, l0[1], C)
                if u == 18:
                    pe.wait_ge(t1_sb, b + 1)
                    square(log_ps, t1, wk, l0[0], C)
                if u == 21:
                    pe.wait_ge(prob_sb, b + 1)
                    square(r_ps, prob, wo, l0[1], C)
                if u == 22:
                    pe.wait_ge(r_sb, b + 1)
                    for m in range(2):
                        o = l0[0][:, m * C:(m + 1) * C]
                        pe.matmul(o, wv[:, 0, m * P:(m + 1) * P], rmat[:, 0], start=True, stop=False)
                        mm = pe.matmul(o, wv[0:CB, 1, m * P:(m + 1) * P], rmat[0:CB, 1], start=False, stop=True)
                    mm.then_inc(mt_ps, 1)
                if 23 <= u < 27:
                    apply_m(u - 23, b)
                if u == 29:
                    group_stats(1, b)
                if 35 <= u < 39:
                    offset_conv(2 * (u - 35), b, par)
                    offset_conv(2 * (u - 35) + 1, b, par)
                if u == 43:
                    offset_max(b)

            def z_group(g, b, par):
                if g == 0:
                    pe.wait_ge(x2_moved, b + 1)
                if g > 0 or not first(b):
                    pe.wait_ge(z_lo, ZG * b + g)
                z_product(tile_at(g // 3, par), g % 3, par).then_inc(z_ps, 1)

            def z_product(j, ky, par):
                row = 4 * j + ky - 3 + PAD_T
                at = lambda k: x2w[k][:, par, ky * W:(ky + ROWS_T) * W] if j == 0 else \
                    x2[k][:, par, row * W:(row + ROWS_T) * W]
                for half in range(2):
                    o = zps[:, half, 0:KO // 2]
                    n = slice(half * KO // 2, (half + 1) * KO // 2)
                    pe.matmul(o, at(0), wpr_h[:, 0, ky, n], start=True, stop=False)
                    pe.matmul(o, at(0), wpr_l[:, 0, ky, n], start=False, stop=False)
                    pe.matmul(o, at(1), wpr_h[:, 0, ky, n], start=False, stop=False)
                    pe.matmul(o, at(2), wpr_h[:, 1, ky, n], start=False, stop=False)
                    mm = pe.matmul(o, at(2), wpr_l[:, 1, ky, n], start=False, stop=True)
                return mm

            def turn_s(u, b):
                t, ky, c = u // 6, u % 6 // 2, u % 2
                if c == 0:
                    pe.wait_ge(st_made, 24 * b + 3 * t + ky + 1)
                if u >= 2 or not first(b):
                    pe.wait_ge(s_lo, UNITS * b + u - 1)
                g = (3 * t + ky) % ST_RING
                for kx in range(3):
                    mm = pe.transpose(sps[u % 2][:, kx * P:(kx + 1) * P], sT[:, g, kx, c * P:(c + 1) * P], eye32[:, :])
                mm.then_inc(s_ps, 1)

            def convolve(u, b, par):
                i, ky, c = u // 6, u % 6 // 2, u % 2
                pe.wait_ge(s_lo, UNITS * b + u + 1)
                if i + c < CHUNKS and (c == 1 or i == 0):
                    pe.wait_ge(z_lo, ZG * b + 3 * (i + c) + ky + 1)
                if u % 6 == 0 and (i > 0 or not first(b)):
                    pe.wait_ge(y_pm, TILES * b + i)
                s_product(u, tile_at(i + c, par), ky, u % 6 == 0, u % 6 == 5).then_inc(sz_done, 1)

            def s_product(u, j, ky, start, stop):
                for kx in range(3):
                    z = slice(kx * C, (kx + 1) * C)
                    s_h, s_l = sh[:, u % S_RING, kx], sl[:, u % S_RING, kx]
                    pe.matmul(acc[:, 0:C], s_h, zh[:, j, ky, z], start=start and kx == 0, stop=False)
                    pe.matmul(acc[:, 0:C], s_h, zl[:, j, ky, z], start=False, stop=False)
                    mm = pe.matmul(acc[:, 0:C], s_l, zh[:, j, ky, z], start=False, stop=stop and kx == 2)
                return mm

            def turn_y(q, b):
                pe.wait_ge(y_pm, TILES * b + 2 * q + 2)
                if q > 0 or not first(b):
                    pe.wait_ge(y_ch, 4 * b + q)
                for i in range(2):
                    y = ypm[:, (2 * q + i) % 4]
                    pe.transpose(yt[:, i * P:(i + 1) * P], y[:, 0:P], eye32[:, :])
                    mm = pe.transpose(yt[:, (2 + i) * P:(3 + i) * P], y[:, P:2 * P], eye32[:, :])
                mm.then_inc(yt_ps, 1)

            def far_pass(b, par, more):
                pe.wait_ge(s_lo, UNITS * (b + 1))
                pe.wait_ge(y_ch, 4 * (b + 1))
                pe.wait_ge(y_pm, TILES * (b + 1))

                def first_chunks(of, n):
                    for g in range(AHEAD):
                        if n + g:
                            pe.wait_ge(fz_lo, FAR_Z * b + n + g)
                        z_product(tile_at(g // 3, 1 - par), g % 3, of).then_inc(fz_ps, 1)

                if more:
                    pe.wait_ge(z_lo, ZG * (b + 1) + AHEAD)
                    first_chunks(par, 0)
                    pe.wait_ge(fz_lo, FAR_Z * b + AHEAD)
                for t in range(TILES):
                    for ky in range(3):
                        pe.wait_ge(f_st, 24 * b + 3 * t + ky + 1)
                        for v in far_of(t, ky):
                            f = far_units[v][2]
                            if v >= 2:
                                pe.wait_ge(fs_lo, FAR_UNITS * b + v - 1)
                            for kx in range(3):
                                mm = pe.transpose(sps[v % 2][:, kx * P:(kx + 1) * P],
                                                  sTf[:, kx, f * P:(f + 1) * P], eye32[:, :])
                            mm.then_inc(fs_ps, 1)
                            pe.wait_ge(fs_lo, FAR_UNITS * b + v + 1)
                            start = ky == 0 and v == far_of(t, 0)[0]
                            if start and t:
                                pe.wait_ge(fy_pm, TILES * b + t)
                            s_product(v, (t + FAR[f]) % CHUNKS, ky, start, v == far_of(t, 2)[-1])\
                                .then_inc(fsz_done, 1)
                    pe.wait_ge(fy_pm, TILES * b + t + 1)
                    if t:
                        pe.wait_ge(fy_ch, TILES * b + t)
                    for m in range(2):
                        mm = pe.transpose(yt[:, m * P:(m + 1) * P], ypm[:, t % 4, m * P:(m + 1) * P], eye32[:, :])
                    mm.then_inc(fyt_ps, 1)
                if more:
                    first_chunks(1 - par, AHEAD)
                    pe.wait_ge(fz_lo, FAR_Z * (b + 1))
                pe.wait_ge(fy_ch, TILES * (b + 1))

            def part1(b, par, more):
                if first(b):
                    for g in range(AHEAD):
                        z_group(g, b, par)
                turn_s(0, b)
                turn_s(1, b)
                for u in range(UNITS):
                    g = u // 2 + AHEAD
                    if u % 2 == 0 and g < ZG:
                        z_group(g, b, par)
                    elif u % 2 == 0 and more:
                        z_group(g - ZG, b + 1, 1 - par)
                    if u + 2 < UNITS:
                        turn_s(u + 2, b)
                    convolve(u, b, par)
                    if u % 12 == 2 and u > 12:
                        turn_y(u // 12 - 1, b)
                    if more:
                        part0(u, b + 1, 1 - par)
                turn_y(3, b)
                where_far(pe, b, par, more, far_pass, (fz_ps, FAR_Z), (fs_ps, FAR_UNITS), (fsz_done, FAR_UNITS),
                          (fyt_ps, TILES))

            wq, wk = wqk[:, :, 0:C], wqk[:, :, C:2 * C]
            images((part0, part1, prepare), pe)

        @block.scalar
        def _(act):
            act.wait_ge(const_in, CONST_DMAS * 16)
            act.wait_ge(pool_setup, 1)

            def normalize(i, src, hi, n, b):
                if i == 0:
                    act.wait_ge(gn_bias, 2 * b + n + 1)
                    if n == 0 and not first(b):
                        act.wait_ge(mx_ps, 4 * b)
                    if n or not first(b):
                        act.wait_ge(xn_lo, 4 * b + 2 * n)
                act.activation(xn[:, i], src[:, i], ACT.Identity, scale=rstd[:, i:i + 1], bias=nbias[:, i:i + 1])
                act.activation(hi, src[:, i], ACT.Identity, scale=rstd[:, i:i + 1],
                               bias=nbias[:, i:i + 1]).then_inc(xn_hi, 1)

            def copy_blocks(dst, src, n):
                for m in range(2):
                    ins = act.copy(dst[0:ROWS[m], m], src[0:ROWS[m], m * n:(m + 1) * n])
                return ins

            def part0(u, b, par):
                if 6 <= u < 8:
                    normalize(u - 6, xin, (xh_a, xhl_b)[u - 6][:, :], 0, b)
                if 10 <= u < 14:
                    r = u - 10
                    act.wait_ge(xt_ps, 4 * b + r + 1)
                    o = l0[r % 2][:, :].bitcast(F16)
                    act.copy(xt[:, 2 * r:2 * r + 2, :], o[:, 0:6 * P].rearrange("p (t n) -> p t n", t=2))\
                       .then_inc(xt_sb, 1)
                if u == 17:
                    act.wait_ge(t1_ps, b + 1)
                    copy_blocks(t1, l0[1], C).then_inc(t1_sb, 1)
                if u == 19:
                    act.wait_ge(log_max, b + 1)
                    for m in range(2):
                        r = ROWS[m]
                        ins = act.activation(prob[0:r, m], l0[0][0:r, m * C:(m + 1) * C], ACT.Exp, scale=HEAD_SCALE,
                                             bias=nmaxs[0:r, m:m + 1], accum_out=rsum[0:r, m:m + 1])
                    ins.then_inc(prob_exp, 1)
                if u == 21:
                    act.wait_ge(r_ps, b + 1)
                    copy_blocks(rmat, l0[1], C).then_inc(r_sb, 1)
                if u == 22:
                    act.wait_ge(mt_ps, b + 1)
                    mt = l0[0][:, 0:2 * C].rearrange("p (m o) -> p m o", m=2)
                    act.copy(mt_h[:, :, 0:C], mt)
                    act.copy(mt_h[:, :, C:2 * P], mt[:, :, P:C]).then_inc(mt_hi, 1)
                if 30 <= u < 32:
                    if u == 30 and (not isinstance(b, int) or b >= 2):
                        act.wait_ge(sz_done, UNITS * (b - 1))
                    normalize(u - 30, x1, inner(x2[2 * (u - 30)], par), 1, b)
                if u == 40:
                    act.wait_ge(off_sb, b + 1)
                    act.activation(mask[:, par], off[:, par, :, 2 * TAPS:J], ACT.Tanh, scale=0.5)
                    act.wait_ge(d_sb, b + 1)
                    act.activation(ay[:, par], ay[:, par], ACT.Abs)
                    act.drain()
                    act.activation(ay[:, par], ay[:, par], ACT.Relu, scale=-1.0, bias=1.0).then_inc(hat_act, 1)
                if u == 41:
                    act.activation(bx[:, par], bx[:, par], ACT.Abs)
                    act.drain()
                if u == 42:
                    act.activation(bx[:, par], bx[:, par], ACT.Relu, scale=-1.0, bias=1.0).then_inc(bx_made, 1)

            def split_z(g, b, par):
                if g % 3 == 0 and not first(b):
                    act.wait_ge(sz_done, UNITS * (b - 1) + 6 * (last_use(g // 3) + 1))
                act.wait_ge(z_ps, ZG * b + g + 1)
                act.copy(zh[:, tile_at(g // 3, par), g % 3].rearrange("p (h n) -> p h n", h=2),
                         zps[:, :, 0:KO // 2]).then_inc(z_hi, 1)

            def far_pass(b, par, more):
                act.wait_ge(sz_done, UNITS * (b + 1))
                act.wait_ge(yt_ps, 4 * (b + 1))

                def first_chunks(n):
                    for g in range(AHEAD):
                        act.wait_ge(fz_ps, FAR_Z * b + n + g + 1)
                        act.copy(zh[:, tile_at(g // 3, 1 - par), g % 3].rearrange("p (h n) -> p h n", h=2),
                                 zps[:, :, 0:KO // 2]).then_inc(fz_hi, 1)

                if more:
                    first_chunks(0)
                for t in range(TILES):
                    for ky in range(3):
                        for v in far_of(t, ky):
                            act.wait_ge(fs_ps, FAR_UNITS * b + v + 1)
                            if v >= S_RING:
                                act.wait_ge(fsz_done, FAR_UNITS * b + v - S_RING + 1)
                            act.copy(sh[:, v % S_RING].rearrange("p k n -> p (k n)"), sps[v % 2][:, 0:3 * P])\
                               .then_inc(fs_hi, 1)
                    act.wait_ge(fsz_done, FAR_UNITS * b + far_end(t))
                    if t >= 4:
                        act.wait_ge(fyt_ps, TILES * b + t - 3)
                    act.copy(ypm[:, t % 4, 0:C], acc[:, 0:C])
                    act.copy(ypm[:, t % 4, C:2 * P], acc[:, P:C]).then_inc(fy_pm, 1)
                if more:
                    first_chunks(AHEAD)
                act.wait_ge(fyt_ps, TILES * (b + 1))

            def split_s(u, b):
                act.wait_ge(s_ps, UNITS * b + u + 1)
                if u >= S_RING or not first(b):
                    act.wait_ge(sz_done, UNITS * b + u - S_RING + 1)
                act.copy(sh[:, u % S_RING].rearrange("p k n -> p (k n)"), sps[u % 2][:, 0:3 * P]).then_inc(s_hi, 1)

            def part1(b, par, more):
                if first(b):
                    for g in range(AHEAD):
                        split_z(g, b, par)
                split_s(0, b)
                split_s(1, b)
                for u in range(UNITS):
                    g = u // 2 + AHEAD
                    if u % 2 == 0 and g < ZG:
                        split_z(g, b, par)
                    elif u % 2 == 0 and more:
                        split_z(g - ZG, b + 1, 1 - par)
                    if u + 2 < UNITS:
                        split_s(u + 2, b)
                    if u % 6 == 5:
                        t = u // 6
                        act.wait_ge(sz_done, UNITS * b + u + 1)
                        if t >= 4 or not first(b):
                            act.wait_ge(yt_ps, 4 * b + t // 2 - 1)
                        act.copy(ypm[:, t % 4, 0:C], acc[:, 0:C])
                        act.copy(ypm[:, t % 4, C:2 * P], acc[:, P:C]).then_inc(y_pm, 1)
                    if more:
                        part0(u, b + 1, 1 - par)
                where_far(act, b, par, more, far_pass, (fz_hi, FAR_Z), (fs_hi, FAR_UNITS), (fy_pm, TILES))

            images((part0, part1, lambda: None), act)

            act.wait_ge(bn_done, 1)

            def gelu_pair(q, slot):
                act.wait_ge(f_loaded[slot], 64 * (q - slot) + 128)
                for i in range(3):
                    m = i // 2
                    act.activation(fin_y[:, slot, i], fin_y[:, slot, i], ACT.Gelu, scale=ga[:, m:m + 1],
                                   bias=gb[:, m:m + 1]).then_inc(f_gelu, 1)

            with act.Fori(0, NB // 2 - 1, 2) as q:
                gelu_pair(q, 0)
                gelu_pair(q + 1, 1)

        @block.vector
        def _(dve):
            dve.wait_ge(const_in, CONST_DMAS * 16)
            dve.tensor_scalar(cmid[:, :], cy_sb[:, 0:1], -CENTRE, None, ALU.add)
            dve.tensor_copy(eye16[:, :], eye32[:, :]).then_inc(dve_setup, 1)

            def prepare():
                dve.wait_ge(weights_in, 6 * 16)
                for i, stage in enumerate((off_stage, proj_stage)):
                    dve.tensor_reduce(wmaxt[:, i:i + 1], stage, AX.XY, ALU.max, apply_absolute_value=True)
                dve.drain()
                dve.tensor_scalar(wmax[:, :], wmaxt[:, :], 1e-30, 1e30, ALU.max, ALU.min).then_inc(dve_setup, 1)
                dve.wait_ge(pe_setup, 1)
                dve.tensor_reduce(wmaxt[:, :], yt[:, 0:2 * P].rearrange("p (i n) -> p i n", i=2), AX.X, ALU.max)
                dve.drain()
                dve.tensor_scalar(unscale[:, :].bitcast(I32), wmaxt[:, :].bitcast(I32), 0x7F800000, None,
                                  ALU.bitwise_and)
                dve.drain()
                dve.reciprocal(scale[:, :], unscale[:, :])
                dve.drain()
                off3 = lambda i: off_stage[:, i].rearrange("p (k j) -> p k j", k=TAPS)
                splits = [(off_stage[:, i], off3(i), wof[:, i, :, 0], wof[:, i, :, 1], 0) for i in range(2)]
                splits += [(proj_stage[:, i], proj_stage[:, i], flat2(wpr_h)[:, i], flat2(wpr_l)[:, i], 1)
                           for i in range(2)]
                for stage, shaped, w_h, w_l, i in splits:
                    dve.tensor_scalar(stage, stage, scale[:, i:i + 1], None, ALU.mult)
                dve.drain()
                for stage, shaped, w_h, w_l, i in splits:
                    dve.tensor_copy(w_h, shaped)
                dve.drain()
                for stage, shaped, w_h, w_l, i in splits:
                    ins = dve.tensor_tensor(w_l, shaped, w_h, ALU.subtract)
                ins.then_inc(dve_setup, 1)
                dve.wait_ge(dve_setup, 3)

            def channel_stats(i, src):
                for half in range(2):
                    dve.bn_stats(stats[:, i, half], src[:, i, half * 512:half * 512 + 512])
                if i == 0:
                    return
                dve.drain()
                for i in range(2):
                    dve.bn_aggr(mv[:, i], stats[:, i].rearrange("p a b -> p (a b)"))
                dve.drain()
                dve.tensor_tensor(msq[:, :], mv[:, :, 0], mv[:, :, 0], ALU.mult)
                dve.drain()
                dve.tensor_tensor(mv[:, :, 1], mv[:, :, 1], msq[:, :], ALU.add).then_inc(gn_stats, 1)

            def group_variance(n, b):
                dve.wait_ge(gn_group, 2 * b + n + 1)
                if n or not first(b):
                    dve.wait_ge(xn_hi, 4 * b + 2 * n)
                dve.tensor_copy(flat(gmv), l0[0][:, 0:4])
                dve.drain()
                dve.tensor_tensor(msq[:, :], gmv[:, :, 0], gmv[:, :, 0], ALU.mult)
                dve.drain()
                dve.scalar_tensor_tensor(out=gvar[:, :], in0=gmv[:, :, 1], scalar=GN_EPS, in1=msq[:, :],
                                         op0=ALU.add, op1=ALU.subtract).then_inc(gn_var, 1)

            def residue(i, lo, hi, n, b):
                dve.wait_ge(xn_hi, 4 * b + 2 * n + i + 1)
                dve.tensor_tensor(lo, xn[:, 0] if i == 0 else xn[CB:P, 1], hi, ALU.subtract).then_inc(xn_lo, 1)

            def move(k, b, par):
                rows = lambda v: v.rearrange("p (h w) -> p h w", w=W)
                src = rows(inner(x2[k], par))
                dve.tensor_copy(rows(inner(x2s[k], 0))[:, :, 1:W], src[:, :, 0:W - 1])
                dve.tensor_copy(rows(inner(x2s[k], 1))[:, :, 0:W - 1], src[:, :, 1:W])
                seam = rows(x2w[k][:, par])
                dve.tensor_copy(seam[:, 0:WRAP], src[:, H - WRAP:H])
                return dve.tensor_copy(seam[:, WRAP:2 * WRAP], src[:, 0:WRAP])

            def zero_outside(hat, rows, tiles):
                for t in tiles:
                    for ky in range(3):
                        above, below = outside(t, ky, rows)
                        k = t * TAPS + 3 * ky
                        if above:
                            dve.memset(hat[:, k:k + 3, 0:above], 0.0)
                        if below:
                            dve.memset(hat[:, k:k + 3, len(rows) - below:len(rows)], 0.0)

            def part0(u, b, par):
                if u < 2:
                    dve.wait_ge(x_loaded, 48 * b + 48)
                    channel_stats(u, xin)
                if u == 3:
                    group_variance(0, b)
                if u == 8:
                    residue(0, xl_a[:, :], xh_a[:, :], 0, b)
                if u == 9:
                    residue(1, xhl_b[CB:P, :], xhl_b[CB:P, :], 0, b)
                if u == 15:
                    dve.wait_ge(gram_ps, b + 1)
                    for m in range(2):
                        ins = dve.tensor_copy(gram[0:ROWS[m], m], l0[0][0:ROWS[m], m * C:(m + 1) * C])
                    ins.then_inc(gram_sb, 1)
                if u == 18:
                    dve.wait_ge(log_ps, b + 1)
                    for m in range(2):
                        dve.tensor_reduce(nmax[0:ROWS[m], m:m + 1], l0[0][0:ROWS[m], m * C:(m + 1) * C], AX.X,
                                          ALU.max, negate=True)
                    dve.drain()
                    for m in range(2):
                        r = ROWS[m]
                        ins = dve.tensor_scalar(nmaxs[0:r, m:m + 1], nmax[0:r, m:m + 1], HEAD_SCALE, None, ALU.mult)
                    ins.then_inc(log_max, 1)
                if u == 20:
                    dve.wait_ge(prob_exp, b + 1)
                    for m in range(2):
                        dve.reciprocal(rinv[0:ROWS[m], m:m + 1], rsum[0:ROWS[m], m:m + 1])
                    dve.drain()
                    for m in range(2):
                        r = ROWS[m]
                        ins = dve.tensor_scalar(prob[0:r, m], prob[0:r, m], rinv[0:r, m:m + 1], None, ALU.mult)
                    ins.then_inc(prob_sb, 1)
                if u == 22:
                    dve.wait_ge(mt_hi, b + 1)
                    mt = l0[0][:, 0:2 * C].rearrange("p (m o) -> p m o", m=2)
                    dve.tensor_tensor(mt_l[:, :, 0:C], mt, mt_h[:, :, 0:C], ALU.subtract)
                    dve.tensor_tensor(mt_l[:, :, C:2 * P], mt[:, :, P:C], mt_h[:, :, C:2 * P], ALU.subtract)\
                       .then_inc(mt_lo, 1)
                if 23 <= u < 27:
                    q = u - 23
                    m, n = q // 2, slice(q % 2 * 512, q % 2 * 512 + 512)
                    dve.wait_ge(mx_ps, 4 * b + q + 1)
                    if q == 0 and not first(b):
                        dve.wait_ge(x1_stored, 32 * b)
                    dve.scalar_tensor_tensor(out=x1[:, m, n], in0=l0[(q + 1) % 2][:, :], scalar=bo[:, m:m + 1],
                                             in1=xin[:, m, n], op0=ALU.add, op1=ALU.add).then_inc(x1_sb, 1)
                if 26 <= u < 28:
                    dve.wait_ge(x1_sb, 4 * b + 2 * (u - 25))
                    channel_stats(u - 26, x1)
                if u == 29:
                    group_variance(1, b)
                if u == 31:
                    residue(0, inner(x2[1], par), inner(x2[0], par), 1, b)
                    if not first(b):
                        dve.wait_ge(off_ps, b)
                    move(0, b, par)
                if u == 32:
                    residue(1, inner(x2[2], par)[CB:P], inner(x2[2], par)[CB:P], 1, b)
                if u == 33:
                    dve.wait_ge(xn_lo, 4 * b + 4)
                    move(1, b, par)
                if u == 34:
                    move(2, b, par).then_inc(x2_moved, 1)
                if u == 39:
                    dve.wait_ge(off_ps, b + 1)
                    if not isinstance(b, int) or b >= 2:
                        dve.wait_ge(st_made, 24 * (b - 1))
                    halves = l0[1][:, 0:TILES * 2 * J].rearrange("p (t i j) -> p t i j", t=TILES, i=2)
                    dve.scalar_tensor_tensor(out=off[:, par], in0=halves[:, :, 0], scalar=unscale[:, 0:1],
                                             in1=boff[:, :, :], op0=ALU.mult, op1=ALU.add)
                    dve.drain()
                    dve.scalar_tensor_tensor(out=off[:, par], in0=halves[:, :, 1], scalar=unscale[:, 0:1],
                                             in1=off[:, par], op0=ALU.mult, op1=ALU.add)
                    dve.drain()
                    yx = off[:, par, :, 0:2 * TAPS]
                    dve.tensor_scalar(yx, yx, -MAX_OFF, MAX_OFF, ALU.max, ALU.min).then_inc(off_sb, 1)
                    dve.wait_ge(off_sb, b + 1)
                    dve.tensor_tensor(hat4(ay, par, R), spread(off[:, par, :, 0:TAPS], R),
                                      cy_sb[:, None, None, 0:R].broadcast_to([P, TILES, TAPS, R]), ALU.add)
                if u == 40:
                    dve.tensor_tensor(hat4(bx, par, W), spread(off[:, par, :, TAPS:2 * TAPS], W),
                                      cx_sb[:, None, :, :].broadcast_to([P, TILES, TAPS, W]), ALU.add)\
                       .then_inc(d_sb, 1)
                if u == 41:
                    dve.tensor_scalar(ypos[:, :, :], off[:, par, :, 0:TAPS], cmid[:, 0:1], None, ALU.add)
                    dve.drain()
                    dve.tensor_reduce(offmax[:, :], ypos[:, :, :], AX.XY, ALU.max,
                                      apply_absolute_value=True).then_inc(omax_sb, 1)
                    dve.wait_ge(hat_act, b + 1)
                    zero_outside(ay[:, par], NEAR_ROWS, (0, TILES - 1))
                    dve.tensor_scalar(mask[:, par], mask[:, par], 1.0, None, ALU.add)
                    dve.drain()
                    dve.tensor_tensor(hat4(ay, par, R), hat4(ay, par, R), spread(mask[:, par], R), ALU.mult)\
                       .then_inc(hats, 1)
                if u == 44:
                    dve.wait_ge(omax_ps, b + 1)
                    dve.tensor_reduce(offmaxg[:, :], l0[0][:, 0:P], AX.X, ALU.max)
                    dve.drain()
                    dve.tensor_scalar(far[:, par:par + 1], offmaxg[:, :], CENTRE, None, ALU.is_gt).then_inc(flag_sb, 1)

            def split_z(g, b, par):
                dve.wait_ge(z_hi, ZG * b + g + 1)
                half = lambda t: t[:, tile_at(g // 3, par), g % 3].rearrange("p (h n) -> p h n", h=2)
                dve.tensor_tensor(half(zl), zps[:, :, 0:KO // 2], half(zh), ALU.subtract).then_inc(z_lo, 1)

            def split_s(u, b):
                dve.wait_ge(s_hi, UNITS * b + u + 1)
                one = lambda t: t[:, u % S_RING].rearrange("p k n -> p (k n)")
                dve.tensor_tensor(one(sl), sps[u % 2][:, 0:3 * P], one(sh), ALU.subtract).then_inc(s_lo, 1)

            def far_pass(b, par, more):
                n_rows = len(FAR_ROWS)
                rows4 = ayf.rearrange("p (t k) r -> p t k r", t=TILES)
                dve.tensor_tensor(rows4, spread(off[:, par, :, 0:TAPS], n_rows),
                                  cy_sb[:, None, None, R:R + n_rows].broadcast_to([P, TILES, TAPS, n_rows]),
                                  ALU.add)
                dve.drain()
                dve.scalar_tensor_tensor(out=ayf, in0=ayf, scalar=-1.0, in1=ayf, op0=ALU.mult, op1=ALU.min)
                dve.drain()
                dve.tensor_scalar(ayf, ayf, 1.0, 0.0, ALU.add, ALU.max)
                dve.drain()
                dve.tensor_tensor(rows4, rows4, spread(mask[:, par], n_rows), ALU.mult)
                dve.drain()
                zero_outside(ayf, FAR_ROWS, range(TILES))
                dve.drain()

                def first_chunks(n):
                    for g in range(AHEAD):
                        dve.wait_ge(fz_hi, FAR_Z * b + n + g + 1)
                        half = lambda v: v[:, tile_at(g // 3, 1 - par), g % 3].rearrange("p (h n) -> p h n", h=2)
                        dve.tensor_tensor(half(zl), zps[:, :, 0:KO // 2], half(zh), ALU.subtract).then_inc(fz_lo, 1)

                if more:
                    first_chunks(0)
                for t in range(TILES):
                    for ky in range(3):
                        v0 = far_of(t, ky)[0]
                        if v0:
                            dve.wait_ge(fs_ps, FAR_UNITS * b + v0)
                        k = t * TAPS + 3 * ky
                        for kx in range(3):
                            ins = dve.tensor_tensor(
                                sTf[:, kx].rearrange("p (r x) -> p r x", r=n_rows),
                                ayf[:, k + kx, :, None].broadcast_to([P, n_rows, W]),
                                bx[:, par, k + kx, None, :].broadcast_to([P, n_rows, W]), ALU.mult)
                        ins.then_inc(f_st, 1)
                        for v in far_of(t, ky):
                            dve.wait_ge(fs_hi, FAR_UNITS * b + v + 1)
                            one = lambda w: w[:, v % S_RING].rearrange("p k n -> p (k n)")
                            dve.tensor_tensor(one(sl), sps[v % 2][:, 0:3 * P], one(sh), ALU.subtract)\
                               .then_inc(fs_lo, 1)
                    dve.wait_ge(fyt_ps, TILES * b + t + 1)
                    for m in range(2):
                        y = ych[:, m, t * P:(t + 1) * P]
                        ins = dve.scalar_tensor_tensor(out=y, in0=yt[:, m * P:(m + 1) * P], scalar=unscale[:, 1:2],
                                                       in1=y, op0=ALU.mult, op1=ALU.add)
                    ins.then_inc(fy_ch, 1)
                if more:
                    first_chunks(AHEAD)

            def scale_y(q, b, par):
                dve.wait_ge(yt_ps, 4 * b + q + 1)
                if q == 0 and not first(b):
                    dve.wait_ge(y_stored, 32 * b)
                n = tile_at(2 * q, par) * P
                for m in range(2):
                    ins = dve.tensor_scalar(ych[:, m, n:n + 2 * P], yt[:, m * 2 * P:(m + 1) * 2 * P],
                                            unscale[:, 1:2], pb[:, m:m + 1], ALU.mult, ALU.add)
                ins.then_inc(y_ch, 1)

            def part1(b, par, more):
                if first(b):
                    for g in range(AHEAD):
                        split_z(g, b, par)
                split_s(0, b)
                split_s(1, b)
                for u in range(UNITS):
                    g = u // 2 + AHEAD
                    if u % 2 == 0 and g < ZG:
                        split_z(g, b, par)
                    elif u % 2 == 0 and more:
                        split_z(g - ZG, b + 1, 1 - par)
                    if u + 2 < UNITS:
                        split_s(u + 2, b)
                    if u % 12 == 3 and u > 12:
                        scale_y(u // 12 - 1, b, par)
                    if more:
                        part0(u, b + 1, 1 - par)
                scale_y(3, b, par)
                where_far(dve, b, par, more, far_pass, (fz_lo, FAR_Z), (f_st, 3 * TILES), (fs_lo, FAR_UNITS),
                          (fy_ch, TILES))
                dve.drain()
                for m in range(2):
                    for half in range(2):
                        ins = dve.bn_stats(ystats[:, m, bass.ds(2 * b + half, 1), :],
                                           ych[:, m, half * 512:(half + 1) * 512])
                ins.then_inc(y_final, 1)

            images((part0, part1, prepare), dve)

            dve.wait_ge(y_final, NB)
            for m in range(2):
                dve.bn_aggr(ymv[:, m], ystats[:, m].rearrange("p a b -> p (a b)"))
            dve.drain()
            dve.tensor_scalar(yvar[:, :], ymv[:, :, 1], BN_EPS, None, ALU.add).then_inc(bn_var, 1)
            dve.wait_ge(bn_rstd, 1)
            dve.tensor_tensor(ga[:, :], gam[:, :], yrstd[:, :], ALU.mult)
            dve.drain()
            dve.tensor_tensor(gmean[:, :], ymv[:, :, 0], ga[:, :], ALU.mult)
            dve.drain()
            dve.tensor_tensor(gb[:, :], bet[:, :], gmean[:, :], ALU.subtract).then_inc(bn_done, 1)

            def add_pair(q, slot):
                for i in range(3):
                    dve.wait_ge(f_gelu, 3 * q + i + 1)
                    dve.tensor_tensor(fin_y[:, slot, i], fin_y[:, slot, i], fin_x[:, slot, i], ALU.add)\
                       .then_inc(f_sum, 1)

            with dve.Fori(0, NB // 2 - 1, 2) as q:
                add_pair(q, 0)
                add_pair(q + 1, 1)

        @block.gpsimd
        def _(pool):
            pool.memset(mhalf[:, :], -0.5)
            pool.memset(minus[:, :], -1.0)
            for t in (*x2, *x2s):
                ins = pool.memset(t[:, :, :], 0.0)
            ins.then_inc(pool_setup, 1)
            pool.wait_ge(pool_setup, 1)
            pool.wait_ge(const_in, CONST_DMAS * 16)

            def group_rstd(n, b):
                pool.wait_ge(gn_var, 2 * b + n + 1)
                pool.tensor_tensor(rstd[:, :], gvar[:, :], mhalf[:, :], ALU.pow).then_inc(gn_rstd, 1)
                pool.wait_ge(gn_rstd, 2 * b + n + 1)
                pool.tensor_tensor(nbias[:, :], gmv[:, :, 0], rstd[:, :], ALU.mult).then_inc(gn_mean, 1)
                pool.wait_ge(gn_mean, 2 * b + n + 1)
                pool.tensor_tensor(nbias[:, :], nbias[:, :], minus[:, :], ALU.mult).then_inc(gn_bias, 1)

            def part0(u, b, par):
                if u == 4:
                    group_rstd(0, b)
                if u == 30:
                    group_rstd(1, b)

            def part1(b, par, more):
                for p in range(3 * TILES):
                    t, ky = tile_at(p // 3, par), p % 3
                    if p == 0:
                        pool.wait_ge(hats, b + 1)
                        pool.wait_ge(bx_made, b + 1)
                    if p >= ST_RING or not first(b):
                        pool.wait_ge(s_ps, UNITS * b + 2 * (p - ST_RING) + 2)
                    k = t * TAPS + 3 * ky
                    a = ay[:, par, k:k + 3, :, None].broadcast_to([P, 3, R, W])
                    x_ = bx[:, par, k:k + 3, None, :].broadcast_to([P, 3, R, W])
                    pool.tensor_tensor(sT[:, p % ST_RING].rearrange("p k (r x) -> p k r x", r=R), a, x_, ALU.mult)\
                        .then_inc(st_made, 1)
                    if more:
                        for u in (2 * p - 4, 2 * p - 3):
                            part0(u, b + 1, 1 - par)

            images((part0, part1, lambda: None), pool)

            pool.wait_ge(bn_var, 1)
            pool.tensor_tensor(yrstd[:, :], yvar[:, :], mhalf[:, :], ALU.pow).then_inc(bn_rstd, 1)

            def store_pair(q, slot):
                pool.wait_ge(f_sum, 3 * q + 3)
                for i in range(2):
                    pool.dma_start(out[2 * q + i, 0:P], fin_y[:, slot, i]).then_inc(f_stored[slot], 16)
                    pool.dma_start(out[2 * q + i, P:C], fin_y[CB * i:CB * i + CB, slot, 2]).then_inc(f_stored[slot], 16)

            with pool.Fori(0, NB // 2 - 1, 2) as q:
                store_pair(q, 0)
                store_pair(q + 1, 1)
            for i in range(2):
                pool.wait_ge(f_stored[i], 16 * NB)

    return nc


def kernel(x, L0_conv_w_qkv, L0_conv_w_out, L0_conv_b_out, L1_conv_proj_w, L1_conv_proj_b, L1_conv_off_w,
           L1_conv_off_b, L1_conv_mask_w, L1_conv_mask_b, L1_conv_gamma, L1_conv_beta):
    import concourse.bacc as bacc
    from concourse.bass_utils import run_bass_kernel_spmd as run

    x = np.asarray(x)
    nb = x.shape[0]
    w_qkv = np.asarray(L0_conv_w_qkv)
    w_off = np.asarray(L1_conv_off_w)
    taps_last = lambda w: np.transpose(w, (1, 2, 3, 0))
    w_27 = np.concatenate([w_off[0::2], w_off[1::2], np.asarray(L1_conv_mask_w)], axis=0)
    b_off = np.asarray(L1_conv_off_b)
    b_27 = np.concatenate([b_off[0::2], b_off[1::2], np.asarray(L1_conv_mask_b)], axis=0)
    avg, cy, cx, eye = coordinate_tables()
    arrays = {
        "x": x.reshape(nb, C, N),
        "w_qkT": w_qkv[0:2 * C].T,
        "w_v": w_qkv[2 * C:3 * C],
        "w_outT": np.asarray(L0_conv_w_out).T,
        "b_out": np.asarray(L0_conv_b_out),
        "w_off": taps_last(w_27).reshape(C, TAPS * J),
        "b_off": b_27,
        "w_proj": taps_last(np.asarray(L1_conv_proj_w)).reshape(C, TAPS * C),
        "proj_b": np.asarray(L1_conv_proj_b),
        "gamma": np.asarray(L1_conv_gamma),
        "beta": np.asarray(L1_conv_beta),
        "avg": avg, "cy": cy, "cx": cx, "eye": eye,
    }
    nc = bacc.Bacc("TRN2", target_bir_lowering=False, num_devices=1)
    arrays = {f"in_{k}": np.ascontiguousarray(v) for k, v in arrays.items()}
    args = [nc.dram_tensor(k, v.shape, mybir.dt.from_np(v.dtype), kind="ExternalInput").ap()
            for k, v in arrays.items()]
    args.append(nc.dram_tensor("out", (nb, C, N), F32, kind="ExternalOutput").ap())
    build(nc, *args)
    r = run(nc, [arrays], core_ids=[0])
    return r.results[0]["out"].reshape(nb, C, H, W)
```

```python
from contextlib import ExitStack

import numpy as np
import concourse.bass as bass
from concourse import mybir

F32, F16, I32 = mybir.dt.float32, mybir.dt.float16, mybir.dt.int32
ALU = mybir.AluOpType
ACT = mybir.ActivationFunctionType
AX = mybir.AxisListType

P = 128
C, H, W = 192, 32, 32
N = H * W
CB = C - P
TAPS = 9
J = 3 * TAPS
GROUPS = 32
ROWS_T = P // W
TILES = N // P
CHUNKS = TILES
R = 2 * ROWS_T
CENTRE = (R - 1) / 2
MAX_OFF = float(min(H, W) // 4)
PAD_T, PAD_ROWS = 1, H + 2
WRAP = 3
KO = 3 * C
UNITS = 6 * TILES
HEAD_SCALE = float((C // 4) ** (-0.5))
GN_EPS = 1e-5
BN_EPS = 1e-5
FAR = [-2, -1, 2, 3]
NEAR_ROWS = list(range(R))
FAR_ROWS = [ROWS_T * f + r for f in FAR for r in range(ROWS_T)]


def outside(t, ky, rows):
    at = [ROWS_T * t + ky - 3 + r for r in rows]
    return sum(r < 0 for r in at), sum(r >= H for r in at)


def coordinate_tables():
    c = np.concatenate([np.arange(P), np.arange(P, C), np.arange(P, C)])
    g = c // (C // GROUPS)
    avg = np.zeros((P, 4, P), np.float32)
    for fb in range(2):
        for tb in range(2):
            same = g[fb * P:fb * P + P, None] == g[None, tb * P:tb * P + P]
            avg[:, 2 * fb + tb, :] = same * np.float32(1.0 / (C // GROUPS))
    p = np.arange(P)
    cy = (p[:, None] // W + 2 - np.array(NEAR_ROWS + FAR_ROWS)[None, :]).astype(np.float32)
    k = np.arange(TAPS)
    cx = (p[:, None, None] % W - 1 + (k % 3)[None, :, None] - np.arange(W)[None, None, :]).astype(np.float32)
    return avg.reshape(P, -1), cy, cx.reshape(P, -1), np.eye(P, dtype=np.float32)


def build(nc, x, w_qkT, w_v, w_outT, b_out, w_off, b_off, w_proj, proj_b, gamma, beta,
          avg, cy, cx, eye, out):
    NB = x.shape[0]
    nc.disable_value_cache = True
    x1_dram = nc.dram_tensor("x1_scratch", [NB, C, N], F32, kind="Internal").ap()
    y_dram = nc.dram_tensor("y_scratch", [NB, C, N], F32, kind="Internal").ap()

    with ExitStack() as ctx:
        def sb(name, shape, dt=F32):
            return ctx.enter_context(nc.sbuf_tensor(name, shape, dt))

        def bank(name, shape=(P, 512), dt=F32):
            return ctx.enter_context(nc.psum_tensor(name, list(shape), dt))

        def sem(name):
            return ctx.enter_context(nc.semaphore(name))

        avg_sb = sb("avg_sb", [P, 4, P])
        cy_sb = sb("cy_sb", [P, R + len(FAR_ROWS)])
        cx_sb = sb("cx_sb", [P, TAPS, W])
        eye32 = sb("eye32", [P, P])
        eye16 = sb("eye16", [P, P], F16)
        mhalf = sb("mhalf", [P, 2])
        minus = sb("minus", [P, 2])
        wqk = sb("wqk", [P, 2, 2 * C])
        wv = sb("wv", [P, 2, 2 * P])
        wo = sb("wo", [P, 2, C])
        wof = sb("wof", [P, 2, TAPS, 2, J], F16)
        wpr_h = sb("wpr_h", [P, 2, 3, KO], F16)
        wpr_l = sb("wpr_l", [P, 2, 3, KO], F16)
        bo = sb("bo", [P, 2])
        pb = sb("pb", [P, 2])
        gam = sb("gam", [P, 2])
        bet = sb("bet", [P, 2])
        boff = sb("boff", [P, TILES, J])
        wmax = sb("wmax", [P, 2])
        wmaxt = sb("wmaxt", [P, 2])
        unscale = sb("unscale", [P, 2])
        scale = sb("scale", [P, 2])
        xin = sb("xin", [P, 2, N])
        xn = sb("xn", [P, 2, N])
        x1 = sb("x1", [P, 2, N])
        stats = sb("stats", [P, 2, 2, 6])
        mv = sb("mv", [P, 2, 2])
        msq = sb("msq", [P, 2])
        gmv = sb("gmv", [P, 2, 2])
        gvar = sb("gvar", [P, 2])
        rstd = sb("rstd", [P, 2])
        nbias = sb("nbias", [P, 2])
        xh_a = sb("xh_a", [P, N], F16)
        xl_a = sb("xl_a", [P, N], F16)
        xhl_b = sb("xhl_b", [P, N], F16)
        xt = sb("xt", [P, TILES, 2 * C], F16)
        gram = sb("gram", [P, 2, C])
        prob = gram
        t1 = sb("t1", [P, 2, C])
        rmat = sb("rmat", [P, 2, C])
        mt_h = sb("mt_h", [P, 2, 2 * P], F16)
        mt_l = sb("mt_l", [P, 2, 2 * P], F16)
        nmax = sb("nmax", [P, 2])
        nmaxs = sb("nmaxs", [P, 2])
        rsum = sb("rsum", [P, 2])
        rinv = sb("rinv", [P, 2])
        x2s = [sb(f"x2s_{n}", [P, 2, PAD_ROWS * W], F16) for n in ("hi_a", "lo_a", "hilo_b")]
        x2w = [sb(f"x2w_{n}", [P, 2, 2 * WRAP * W], F16) for n in ("hi_a", "lo_a", "hilo_b")]
        x2 = [sb(f"x2_{n}", [P, 2, PAD_ROWS * W], F16) for n in ("hi_a", "lo_a", "hilo_b")]
        off = sb("off", [P, 2, TILES, J])
        ay = sb("ay", [P, 2, TILES * TAPS, R])
        bx = sb("bx", [P, 2, TILES * TAPS, W])
        mask = sb("mask", [P, 2, TILES, TAPS])
        cmid = sb("cmid", [P, 1])
        ypos = sb("ypos", [P, TILES, TAPS])
        offmax = sb("offmax", [P, 1])
        offmaxg = sb("offmaxg", [P, 1])
        far = sb("far", [P, 2], I32)
        zh = sb("zh", [P, CHUNKS, 3, KO], F16)
        zl = sb("zl", [P, CHUNKS, 3, KO], F16)
        ST_RING = 3
        sT = sb("sT", [P, ST_RING, 3, R * W])
        S_RING = 3
        sh = sb("sh", [P, S_RING, 3, P], F16)
        sl = sb("sl", [P, S_RING, 3, P], F16)
        ypm = sb("ypm", [P, 4, 2 * P])
        ych = sb("ych", [P, 2, N])
        ystats = sb("ystats", [P, 2, NB * 2, 6])
        ymv = sb("ymv", [P, 2, 2])
        yvar = sb("yvar", [P, 2])
        yrstd = sb("yrstd", [P, 2])
        ga = sb("ga", [P, 2])
        gmean = sb("gmean", [P, 2])
        gb = sb("gb", [P, 2])

        acc = bank("acc")
        yt = bank("yt")
        zps = bank("zps", (P, 2, 512))
        sps = [bank(f"sps{i}") for i in range(2)]
        l0 = [bank(f"l0_{i}") for i in range(2)]

        const_in = sem("const_in")
        matrices_in = sem("matrices_in")
        weights_in = sem("weights_in")
        dve_setup = sem("dve_setup")
        pool_setup = sem("pool_setup")
        pe_setup = sem("pe_setup")
        x_loaded = sem("x_loaded")
        gn_stats = sem("gn_stats")
        gn_group = sem("gn_group")
        gn_var = sem("gn_var")
        gn_rstd = sem("gn_rstd")
        gn_mean = sem("gn_mean")
        gn_bias = sem("gn_bias")
        xn_hi = sem("xn_hi")
        xn_lo = sem("xn_lo")
        xt_ps = sem("xt_ps")
        xt_sb = sem("xt_sb")
        gram_ps = sem("gram_ps")
        gram_sb = sem("gram_sb")
        gram_t_ps = sem("gram_t_ps")
        gram_t_sb = sem("gram_t_sb")
        t1_ps = sem("t1_ps")
        t1_sb = sem("t1_sb")
        log_ps = sem("log_ps")
        log_max = sem("log_max")
        prob_exp = sem("prob_exp")
        prob_sb = sem("prob_sb")
        r_ps = sem("r_ps")
        r_sb = sem("r_sb")
        mt_ps = sem("mt_ps")
        mt_hi = sem("mt_hi")
        mt_lo = sem("mt_lo")
        mx_ps = sem("mx_ps")
        x1_sb = sem("x1_sb")
        x1_stored = sem("x1_stored")
        x2_moved = sem("x2_moved")
        off_ps = sem("off_ps")
        off_sb = sem("off_sb")
        dy_sb = sem("dy_sb")
        dx_sb = sem("dx_sb")
        hat_act = sem("hat_act")
        bx_made = sem("bx_made")
        hats = sem("hats")
        omax_sb = sem("omax_sb")
        omax_ps = sem("omax_ps")
        flag_sb = sem("flag_sb")
        z_ps = sem("z_ps")
        z_hi = sem("z_hi")
        z_lo = sem("z_lo")
        st_made = sem("st_made")
        s_ps = sem("s_ps")
        s_hi = sem("s_hi")
        s_lo = sem("s_lo")
        sz_done = sem("sz_done")
        y_pm = sem("y_pm")
        yt_ps = sem("yt_ps")
        y_ch = sem("y_ch")
        y_final = sem("y_final")
        y_stored = sem("y_stored")
        fz_ps = sem("fz_ps")
        fz_hi = sem("fz_hi")
        fz_lo = sem("fz_lo")
        f_st = sem("f_st")
        fs_ps = sem("fs_ps")
        fs_hi = sem("fs_hi")
        fs_lo = sem("fs_lo")
        fsz_done = sem("fsz_done")
        fy_pm = sem("fy_pm")
        fyt_ps = sem("fyt_ps")
        fy_ch = sem("fy_ch")
        flag_seen = sem("flag_seen")
        far_left = sem("far_left")
        bn_var = sem("bn_var")
        bn_rstd = sem("bn_rstd")
        bn_done = sem("bn_done")
        f_loaded = [sem(f"f_loaded{i}") for i in range(3)]
        f_gelu = sem("f_gelu")
        f_sum = sem("f_sum")
        f_stored = [sem(f"f_stored{i}") for i in range(3)]

        SLOTS = UNITS
        CONST_DMAS = 4
        MATRIX_DMAS = TILES + 3 + 3 + 4 + 3 * 4

        def flat(t):
            v = t[tuple([slice(None)] * len(t.shape))]
            return v.rearrange("p a b -> p (a b)")

        def flat2(t):
            v = t[:, :, :, :]
            return v.rearrange("p i a b -> p i (a b)")

        def inner(t, par):
            return t[:, par, PAD_T * W:PAD_T * W + N]

        def half_tiles(h, par):
            first_tile = tile_at(h * TILES // 2, par)
            return slice(first_tile, first_tile + TILES // 2)

        def ay_half(h, par):
            return ay[:, par].rearrange("p (t k) n -> p t k n", t=TILES)[:, half_tiles(h, par)]

        def bx_part(q, par):
            k = tile_at(2 * q, par) * TAPS
            return bx[:, par, k:k + 2 * TAPS]

        def spread(v, n):
            return v[:, :, :, None].broadcast_to([P, v.shape[1], TAPS, n])

        zl_flat = zl[:, :, :, :].rearrange("p j k o -> p (j k o)")
        zh_flat = zh[:, :, :, :].rearrange("p j k o -> p (j k o)")
        proj_stage = zl_flat[:, 0:2 * 2 * TAPS * C].bitcast(F32).rearrange("p (i n) -> p i n", i=2)
        off_stage = zh_flat[:, 0:2 * 2 * TAPS * J].bitcast(F32).rearrange("p (i n) -> p i n", i=2)
        ayf = xn[:, :, :].rearrange("p a n -> p (a n)")[:, 0:TILES * TAPS * len(FAR_ROWS)]\
            .rearrange("p (k r) -> p k r", r=len(FAR_ROWS))
        sTf = xt[:, :, :].rearrange("p t n -> p (t n)").bitcast(F32).rearrange("p (k m) -> p k m", k=3)
        in_z = lambda v: v[:, 0:2 * 2 * 3 * N].bitcast(F32).rearrange("p (s i n) -> p s i n", s=2, i=3)
        y_in_z, x_in_z = in_z(zh_flat), in_z(zl_flat)
        fin_y = [[xin[:, 0], xin[:, 1], x1[:, 0]]] + [[y_in_z[:, s, i] for i in range(3)] for s in range(2)]
        fin_x = [[x1[:, 1], xn[:, 0], xn[:, 1]]] + [[x_in_z[:, s, i] for i in range(3)] for s in range(2)]
        FIN = len(fin_y)
        PAIRS = NB // 2
        ROUNDS = PAIRS // FIN
        ROUND_ENDS = FIN * ROUNDS

        def all_pairs(eng, step):
            with eng.Fori(0, ROUNDS) as r_:
                for i in range(FIN):
                    step(r_, i)
            for i in range(PAIRS - ROUND_ENDS):
                step(ROUNDS, i)

        def images(program, eng):
            part0, part1, weights_ready = program
            for u in range(SLOTS):
                part0(u, 0, 0)
                if u == 15:
                    weights_ready()
            part1(0, 0, True)
            with eng.Fori(1, NB - 2, 2) as b:
                part1(b, 1, True)
                part1(b + 1, 0, True)
            part1(NB - 1, (NB - 1) % 2, False)

        far_units = [(t, ky, f) for t in range(TILES) for ky in range(3)
                     for f, c in enumerate(FAR) if 0 <= t + c <= CHUNKS]
        FAR_UNITS = len(far_units)
        far_of = lambda t, ky: [v for v, w in enumerate(far_units) if w[0:2] == (t, ky)]
        far_end = lambda t: sum(w[0] <= t for w in far_units)
        AHEAD = 10
        FAR_Z = 2 * AHEAD
        FAR_SLOT = S_RING - 1

        def tile_at(i, par):
            return (i + par * TILES // 2) % TILES

        def z_piece(z, g, par):
            half = g % 2 * (KO // 2)
            return z[:, tile_at(g // 6, par), g % 6 // 2, half:half + KO // 2]

        def last_use(m):
            was = (m + TILES // 2) % TILES
            return was if was else TILES - 1

        def first(b):
            return isinstance(b, int) and b == 0

        ROWS = (P, CB)
        COLS = (slice(0, P), slice(P, C))

        def is_far(eng, b, par):
            eng.wait_ge(flag_sb, b + 1)
            eng.sem_inc(flag_seen, 1)
            return eng.value_load(far[0:1, par:par + 1], min_val=0, max_val=1)

        def where_far(flag, eng, b, par, more, far_pass, *counts):
            with eng.If(flag == 1):
                far_pass(b, par, more)
                eng.sem_inc(far_left, 1)
            with eng.Else():
                for s, n in counts:
                    eng.sem_inc(s, n)

        def load_blocks(eng, dst, src, done):
            eng.dma_start(dst[:, 0], src[0:P]).then_inc(done, 16)
            eng.dma_start(dst[0:CB, 1], src[P:C]).then_inc(done, 16)
            eng.dma_start(dst[CB:P, 1], src[P:C]).then_inc(done, 16)

        block = ctx.enter_context(nc.Block())

        @block.sync
        def _(sp):
            def load_x(b):
                for dst, src in ((xin[:, 0], x[b, 0:P]), (xin[0:CB, 1], x[b, P:C]), (xin[CB:P, 1], x[b, P:C])):
                    sp.dma_start(dst, src).then_inc(x_loaded, 16)

            load_blocks(sp, off_stage, w_off, weights_in)
            load_blocks(sp, proj_stage, w_proj, weights_in)
            sp.dma_start(eye32[:, :], eye).then_inc(const_in, 16)
            load_x(0)
            sp.dma_start(avg_sb[:, :, :], avg.rearrange("p (a b) -> p a b", a=4)).then_inc(const_in, 16)
            sp.dma_start(cy_sb[:, :], cy).then_inc(const_in, 16)
            sp.dma_start(cx_sb[:, :, :], cx.rearrange("p (k x) -> p k x", k=TAPS)).then_inc(const_in, 16)

            def attended(b, more=True):
                sp.wait_ge(x1_sb, 4 * b + 4)
                sp.dma_start(x1_dram[b, 0:P], x1[:, 0]).then_inc(x1_stored, 16)
                sp.dma_start(x1_dram[b, P:C], x1[0:CB, 1]).then_inc(x1_stored, 16)
                if more:
                    load_x(b + 1)

            def convolved(b):
                sp.wait_ge(y_final, b + 1)
                sp.dma_start(y_dram[b, 0:P], ych[:, 0]).then_inc(y_stored, 16)
                sp.dma_start(y_dram[b, P:C], ych[0:CB, 1]).then_inc(y_stored, 16)

            attended(0)
            with sp.Fori(1, NB - 2, 2) as b:
                attended(b)
                convolved(b - 1)
                attended(b + 1)
                convolved(b)
            attended(NB - 1, False)
            convolved(NB - 2)

            def load(dst, src, q, slot, i):
                if i < 2:
                    sp.dma_start(dst[slot][i], src[2 * q + i, 0:P]).then_inc(f_loaded[slot], 16)
                else:
                    for h in range(2):
                        sp.dma_start(dst[slot][i][CB * h:CB * h + CB], src[2 * q + h, P:C])\
                          .then_inc(f_loaded[slot], 16)

            def load_pair(q, slot):
                for i in range(3):
                    load(fin_y, y_dram, q, slot, i)
                    load(fin_x, x1_dram, q, slot, i)

            sp.wait_ge(y_stored, 32 * (NB - 2))
            sp.wait_ge(x1_stored, 32 * NB)
            sp.wait_ge(xn_hi, 4 * NB)
            for i in range(3):
                load(fin_y, y_dram, 0, 0, i)
            load(fin_x, x1_dram, 0, 0, 0)
            convolved(NB - 1)
            sp.wait_ge(bn_var, 1)
            for i in range(1, 3):
                load(fin_x, x1_dram, 0, 0, i)
            for slot in range(1, FIN):
                load_pair(slot, slot)
            sp.wait_ge(y_stored, 32 * NB)

            def load_next(r_, slot):
                sp.wait_ge(f_stored[slot], 64 * r_)
                load_pair(FIN * r_ + slot, slot)

            with sp.Fori(1, ROUNDS) as r_:
                for slot in range(FIN):
                    load_next(r_, slot)
            for slot in range(PAIRS - ROUND_ENDS):
                load_next(ROUNDS, slot)

        @block.tensor
        def _(pe):
            pe.wait_ge(const_in, CONST_DMAS * 16)
            pe.wait_ge(dve_setup, 2)
            pe.wait_ge(pool_setup, 1)
            for i in range(2):
                mm = pe.transpose(yt[:, i * P:(i + 1) * P], wmax[:, i:i + 1].broadcast_to([P, P]), eye32[:, :])
            mm.then_inc(pe_setup, 1)

            def weights_ready():
                pe.wait_ge(matrices_in, MATRIX_DMAS * 16)
                pe.wait_ge(dve_setup, 3)

            def group_stats(n, b):
                pe.wait_ge(gn_stats, 2 * b + n + 1)
                for tb in range(2):
                    o = l0[0][:, 2 * tb:2 * tb + 2]
                    pe.matmul(o, avg_sb[:, tb, :], mv[:, 0, :], start=True, stop=False)
                    mm = pe.matmul(o, avg_sb[0:CB, 2 + tb, :], mv[0:CB, 1, :], start=False, stop=True)
                mm.then_inc(gn_group, 1)

            def square(done, lhs, rhs, ps, n):
                for m in range(2):
                    o = ps[0:ROWS[m], m * n:(m + 1) * n]
                    pe.matmul(o, lhs[:, 0, COLS[m]], rhs[:, 0], start=True, stop=False)
                    mm = pe.matmul(o, lhs[0:CB, 1, COLS[m]], rhs[0:CB, 1], start=False, stop=True)
                mm.then_inc(done, 1)

            def transpose_x(r, b):
                if r == 0:
                    pe.wait_ge(xn_lo, 4 * b + 2)
                if r >= 2:
                    pe.wait_ge(xt_sb, 4 * b + r - 1)
                o = l0[r % 2][:, :].bitcast(F16)
                for i in range(2):
                    n = slice((2 * r + i) * P, (2 * r + i + 1) * P)
                    for k, src in enumerate((xh_a, xhl_b, xl_a)):
                        mm = pe.transpose(o[:, i * 3 * P + k * P:i * 3 * P + (k + 1) * P], src[:, n], eye16[:, :])
                mm.then_inc(xt_ps, 1)

            def gram_product(b):
                pe.wait_ge(xt_sb, 4 * b + 4)
                o, corner = l0[0][:, 0:C], l0[0][0:CB, C + P:2 * C]
                for t in range(TILES):
                    hi, lo_b, lo_a = xt[:, t, 0:C], xt[:, t, C:2 * P], xt[:, t, 2 * P:3 * P]
                    pe.matmul(o, hi[:, 0:P], hi, start=(t == 0), stop=False)
                    pe.matmul(o[:, 0:P], hi[:, 0:P], lo_a, start=False, stop=False)
                    pe.matmul(o[:, P:C], hi[:, 0:P], lo_b, start=False, stop=False)
                    pe.matmul(o, lo_a, hi, start=False, stop=(t == TILES - 1))
                for t in range(TILES):
                    hi_b, lo_b = xt[:, t, P:C], xt[:, t, C:2 * P]
                    pe.matmul(corner, hi_b, hi_b, start=(t == 0), stop=False)
                    pe.matmul(corner, hi_b, lo_b, start=False, stop=False)
                    mm = pe.matmul(corner, lo_b, hi_b, start=False, stop=(t == TILES - 1))
                mm.then_inc(gram_ps, 1)

            def gram_times_wq(b):
                pe.wait_ge(gram_sb, b + 1)
                for m in (1, 0):
                    o = l0[1][0:ROWS[m], m * C:(m + 1) * C]
                    pe.matmul(o, gram[:, 0, COLS[m]], wq[:, 0], start=True, stop=False)
                    if m == 1:
                        pe.transpose(l0[0][0:CB, 2 * C:2 * C + P], gram[:, 0, P:C], eye32[:, :])\
                          .then_inc(gram_t_ps, 1)
                    if m == 0:
                        pe.wait_ge(gram_t_sb, b + 1)
                    mm = pe.matmul(o, gram[0:CB, 1, COLS[m]], wq[0:CB, 1], start=False, stop=True)
                mm.then_inc(t1_ps, 1)

            def apply_m(q, b):
                m, half = divmod(q, 2)
                if q == 0:
                    pe.wait_ge(mt_lo, b + 1)
                if q >= 2:
                    pe.wait_ge(x1_sb, 4 * b + q - 1)
                o = l0[(q + 1) % 2][:, :]
                n = slice(half * 512, half * 512 + 512)
                pe.matmul(o, mt_h[:, 0, m * P:(m + 1) * P], xh_a[:, n], start=True, stop=False)
                pe.matmul(o, mt_h[:, 0, m * P:(m + 1) * P], xl_a[:, n], start=False, stop=False)
                pe.matmul(o, mt_l[:, 0, m * P:(m + 1) * P], xh_a[:, n], start=False, stop=False)
                pe.matmul(o, mt_h[:, 1, m * P:(m + 1) * P], xhl_b[:, n], start=False, stop=False)
                pe.matmul(o, mt_l[:, 1, m * P:(m + 1) * P], xhl_b[:, n], start=False, stop=True).then_inc(mx_ps, 1)

            def offset_conv(t, b, par):
                if t == 0:
                    pe.wait_ge(x2_moved, b + 1)
                o = l0[1][:, t * 2 * J:(t + 1) * 2 * J]
                for k in range(TAPS):
                    row = ROWS_T * t + k // 3 - 1 + PAD_T
                    for n, (plane, m) in enumerate(((0, 0), (1, 0), (2, 1))):
                        src = x2[plane][:, par] if k % 3 == 1 else x2s[plane][:, k % 3 // 2]
                        mm = pe.matmul(o, src[:, row * W:(row + ROWS_T) * W],
                                       wof[:, m, k].rearrange("p i j -> p (i j)"),
                                       start=(k == 0 and n == 0), stop=(k == TAPS - 1 and n == 2))
                if t == TILES - 1:
                    mm.then_inc(off_ps, 1)

            def offset_max(b):
                pe.wait_ge(omax_sb, b + 1)
                if not first(b):
                    pe.wait_ge(y_ch, 4 * b)
                pe.transpose(yt[:, 0:P], offmax[:, :].broadcast_to([P, P]), eye32[:, :]).then_inc(omax_ps, 1)

            def part0(u, b, par):
                if u == 4:
                    group_stats(0, b)
                if 12 <= u < 16:
                    transpose_x(u - 12, b)
                if u == 16:
                    gram_product(b)
                if u == 17:
                    gram_times_wq(b)
                if u == 18:
                    pe.wait_ge(t1_sb, b + 1)
                    square(log_ps, t1, wk, l0[0], C)
                if u == 21:
                    pe.wait_ge(prob_sb, b + 1)
                    square(r_ps, prob, wo, l0[1], C)
                if u == 22:
                    pe.wait_ge(r_sb, b + 1)
                    for m in range(2):
                        o = l0[0][:, m * C:(m + 1) * C]
                        pe.matmul(o, wv[:, 0, m * P:(m + 1) * P], rmat[:, 0], start=True, stop=False)
                        mm = pe.matmul(o, wv[0:CB, 1, m * P:(m + 1) * P], rmat[0:CB, 1], start=False, stop=True)
                    mm.then_inc(mt_ps, 1)
                if 23 <= u < 27:
                    apply_m(u - 23, b)
                if u == 28:
                    group_stats(1, b)
                if 38 <= u < 40:
                    for t in range(TILES // 2):
                        offset_conv(TILES // 2 * (u - 38) + t, b, par)

            def z_group(g, b, par):
                if g == 0:
                    pe.wait_ge(x2_moved, b + 1)
                if g >= 2 or not first(b):
                    pe.wait_ge(z_lo, UNITS * b + g - 1)
                z_product(g, par, par).then_inc(z_ps, 1)

            def z_product(g, par, of):
                j, ky = tile_at(g // 6, par), g % 6 // 2
                row = 4 * j + ky - 3 + PAD_T
                at = lambda k: x2w[k][:, of, ky * W:(ky + ROWS_T) * W] if j == 0 else \
                    x2[k][:, of, row * W:(row + ROWS_T) * W]
                o = zps[:, g % 2, 0:KO // 2]
                n = slice(g % 2 * KO // 2, (g % 2 + 1) * KO // 2)
                pe.matmul(o, at(0), wpr_h[:, 0, ky, n], start=True, stop=False)
                pe.matmul(o, at(0), wpr_l[:, 0, ky, n], start=False, stop=False)
                pe.matmul(o, at(1), wpr_h[:, 0, ky, n], start=False, stop=False)
                pe.matmul(o, at(2), wpr_h[:, 1, ky, n], start=False, stop=False)
                return pe.matmul(o, at(2), wpr_l[:, 1, ky, n], start=False, stop=True)

            def turn_s(u, b):
                t, ky, c = u // 6, u % 6 // 2, u % 2
                if c == 0:
                    pe.wait_ge(st_made, 24 * b + 3 * t + ky + 1)
                if u >= 2 or not first(b):
                    pe.wait_ge(s_lo, UNITS * b + u - 1)
                g = (3 * t + ky) % ST_RING
                for kx in range(3):
                    mm = pe.transpose(sps[u % 2][:, kx * P:(kx + 1) * P], sT[:, g, kx, c * P:(c + 1) * P], eye32[:, :])
                mm.then_inc(s_ps, 1)

            def convolve(u, b, par):
                i, ky, c = u // 6, u % 6 // 2, u % 2
                pe.wait_ge(s_lo, UNITS * b + u + 1)
                if i + c < CHUNKS and (c == 1 or i == 0):
                    pe.wait_ge(z_lo, UNITS * b + 6 * (i + c) + 2 * ky + 2)
                if u % 6 == 0 and (i > 0 or not first(b)):
                    pe.wait_ge(y_pm, TILES * b + i)
                s_product(u % S_RING, tile_at(i + c, par), ky, u % 6 == 0, u % 6 == 5).then_inc(sz_done, 1)

            def s_product(slot, j, ky, start, stop):
                for kx in range(3):
                    z = slice(kx * C, (kx + 1) * C)
                    s_h, s_l = sh[:, slot, kx], sl[:, slot, kx]
                    pe.matmul(acc[:, 0:C], s_h, zh[:, j, ky, z], start=start and kx == 0, stop=False)
                    pe.matmul(acc[:, 0:C], s_h, zl[:, j, ky, z], start=False, stop=False)
                    mm = pe.matmul(acc[:, 0:C], s_l, zh[:, j, ky, z], start=False, stop=stop and kx == 2)
                return mm

            def turn_y(q, b):
                pe.wait_ge(y_pm, TILES * b + 2 * q + 2)
                if q == 0:
                    pe.wait_ge(flag_sb, b + 1)
                if q > 0 or not first(b):
                    pe.wait_ge(y_ch, 4 * b + q)
                for i in range(2):
                    y = ypm[:, (2 * q + i) % 4]
                    pe.transpose(yt[:, i * P:(i + 1) * P], y[:, 0:P], eye32[:, :])
                    mm = pe.transpose(yt[:, (2 + i) * P:(3 + i) * P], y[:, P:2 * P], eye32[:, :])
                mm.then_inc(yt_ps, 1)

            def far_pass(b, par, more):
                pe.wait_ge(s_lo, UNITS * (b + 1) + 2 * more)
                pe.wait_ge(y_ch, 4 * (b + 1))
                pe.wait_ge(y_pm, TILES * (b + 1))

                def first_chunks(of, n):
                    for g in range(AHEAD):
                        if n + g >= 2:
                            pe.wait_ge(fz_lo, FAR_Z * b + n + g - 1)
                        z_product(g, 1 - par, of).then_inc(fz_ps, 1)

                if more:
                    pe.wait_ge(z_lo, UNITS * (b + 1) + AHEAD)
                    first_chunks(par, 0)
                    pe.wait_ge(fz_lo, FAR_Z * b + AHEAD)
                for t in range(TILES):
                    for ky in range(3):
                        pe.wait_ge(f_st, 24 * b + 3 * t + ky + 1)
                        for v in far_of(t, ky):
                            f = far_units[v][2]
                            if v >= 2:
                                pe.wait_ge(fs_lo, FAR_UNITS * b + v - 1)
                            for kx in range(3):
                                mm = pe.transpose(sps[v % 2][:, kx * P:(kx + 1) * P],
                                                  sTf[:, kx, f * P:(f + 1) * P], eye32[:, :])
                            mm.then_inc(fs_ps, 1)
                            pe.wait_ge(fs_lo, FAR_UNITS * b + v + 1)
                            start = ky == 0 and v == far_of(t, 0)[0]
                            if start and t:
                                pe.wait_ge(fy_pm, TILES * b + t)
                            s_product(FAR_SLOT, (t + FAR[f]) % CHUNKS, ky, start, v == far_of(t, 2)[-1])\
                                .then_inc(fsz_done, 1)
                    pe.wait_ge(fy_pm, TILES * b + t + 1)
                    if t:
                        pe.wait_ge(fy_ch, TILES * b + t)
                    for m in range(2):
                        mm = pe.transpose(yt[:, m * P:(m + 1) * P], ypm[:, t % 4, m * P:(m + 1) * P], eye32[:, :])
                    mm.then_inc(fyt_ps, 1)
                if more:
                    first_chunks(1 - par, AHEAD)
                    pe.wait_ge(fz_lo, FAR_Z * (b + 1))
                pe.wait_ge(fy_ch, TILES * (b + 1))

            def part1(b, par, more):
                if first(b):
                    for g in range(AHEAD):
                        z_group(g, b, par)
                    turn_s(0, b)
                    turn_s(1, b)
                for u in range(UNITS):
                    if u + 2 < UNITS:
                        turn_s(u + 2, b)
                    elif more:
                        turn_s(u + 2 - UNITS, b + 1)
                    convolve(u, b, par)
                    if u == 9:
                        offset_max(b)
                    if u + AHEAD < UNITS:
                        z_group(u + AHEAD, b, par)
                    elif more:
                        z_group(u + AHEAD - UNITS, b + 1, 1 - par)
                    if u % 12 == 2 and u > 12:
                        turn_y(u // 12 - 1, b)
                    if more:
                        part0(u, b + 1, 1 - par)
                flag = is_far(pe, b, par)
                turn_y(3, b)
                where_far(flag, pe, b, par, more, far_pass, (fz_ps, FAR_Z), (fs_ps, FAR_UNITS), (fsz_done, FAR_UNITS),
                          (fyt_ps, TILES))

            wq, wk = wqk[:, :, 0:C], wqk[:, :, C:2 * C]
            images((part0, part1, weights_ready), pe)

        @block.scalar
        def _(act):
            load_blocks(act, wqk, w_qkT, matrices_in)
            load_blocks(act, wo, w_outT, matrices_in)
            for i in range(2):
                rows = slice(i * P, i * P + ROWS[i])
                act.dma_start(wv[0:ROWS[i], i, 0:C], w_v[rows]).then_inc(matrices_in, 16)
                act.dma_start(wv[0:ROWS[i], i, C:2 * P], w_v[rows, P:C]).then_inc(matrices_in, 16)
            for dst, src in ((bo, b_out), (pb, proj_b), (gam, gamma), (bet, beta)):
                load_blocks(act, dst[:, :, None], src[:, None], matrices_in)
            for t in range(TILES):
                act.dma_start(boff[:, t, :], b_off.partition_broadcast(P)).then_inc(matrices_in, 16)
            act.wait_ge(const_in, CONST_DMAS * 16)
            act.wait_ge(pool_setup, 1)

            def normalize(as_hi, i, src, hi, n, b):
                if as_hi:
                    act.activation(hi, src[:, i], ACT.Identity, scale=rstd[:, i:i + 1],
                                   bias=nbias[:, i:i + 1]).then_inc(xn_hi, 1)
                    return
                if i == 0:
                    act.wait_ge(gn_bias, 2 * b + n + 1)
                    if n == 0 and not first(b):
                        act.wait_ge(mx_ps, 4 * b)
                    if n or not first(b):
                        act.wait_ge(xn_lo, 4 * b + 2 * n)
                act.activation(xn[:, i], src[:, i], ACT.Identity, scale=rstd[:, i:i + 1], bias=nbias[:, i:i + 1])

            def copy_blocks(dst, src, n):
                for m in range(2):
                    ins = act.copy(dst[0:ROWS[m], m], src[0:ROWS[m], m * n:(m + 1) * n])
                return ins

            def part0(u, b, par):
                if 6 <= u < 10:
                    i = (u - 6) // 2
                    normalize(u % 2, i, xin, (xh_a, xhl_b)[i][:, :], 0, b)
                if 12 <= u < 16:
                    r = u - 12
                    act.wait_ge(xt_ps, 4 * b + r + 1)
                    o = l0[r % 2][:, :].bitcast(F16)
                    act.copy(xt[:, 2 * r:2 * r + 2, :], o[:, 0:6 * P].rearrange("p (t n) -> p t n", t=2))\
                       .then_inc(xt_sb, 1)
                if u == 17:
                    act.wait_ge(gram_t_ps, b + 1)
                    act.copy(gram[0:CB, 1, 0:P], l0[0][0:CB, 2 * C:2 * C + P]).then_inc(gram_t_sb, 1)
                    act.wait_ge(t1_ps, b + 1)
                    copy_blocks(t1, l0[1], C).then_inc(t1_sb, 1)
                if u == 19:
                    act.wait_ge(log_max, b + 1)
                    for m in range(2):
                        r = ROWS[m]
                        ins = act.activation(prob[0:r, m], l0[0][0:r, m * C:(m + 1) * C], ACT.Exp, scale=HEAD_SCALE,
                                             bias=nmaxs[0:r, m:m + 1], accum_out=rsum[0:r, m:m + 1])
                    ins.then_inc(prob_exp, 1)
                if u == 21:
                    act.wait_ge(r_ps, b + 1)
                    copy_blocks(rmat, l0[1], C).then_inc(r_sb, 1)
                if u == 22:
                    act.wait_ge(mt_ps, b + 1)
                    mt = l0[0][:, 0:2 * C].rearrange("p (m o) -> p m o", m=2)
                    act.copy(mt_h[:, :, 0:C], mt)
                    act.copy(mt_h[:, :, C:2 * P], mt[:, :, P:C]).then_inc(mt_hi, 1)
                if 30 <= u < 34:
                    if u == 30 and (not isinstance(b, int) or b >= 2):
                        act.wait_ge(sz_done, UNITS * (b - 1))
                    i = (u - 30) // 2
                    normalize(u % 2, i, x1, inner(x2[2 * i], par), 1, b)
                if u == 41:
                    act.wait_ge(off_sb, b + 1)
                    act.activation(mask[:, par], off[:, par, :, 2 * TAPS:J], ACT.Tanh, scale=0.5)
                if u in (41, 45):
                    h = u // 45
                    d = ay_half(h, par).rearrange("p t k n -> p (t k n)")
                    act.wait_ge(dy_sb, 2 * b + h + 1)
                    act.activation(d, d, ACT.Abs)
                    act.drain()
                    act.activation(d, d, ACT.Relu, scale=-1.0, bias=1.0).then_inc(hat_act, 1)
                if u == 42:
                    column_hats(0, b, par)

            def column_hats(q, b, par):
                d = bx_part(q, par)
                act.wait_ge(dx_sb, 4 * b + q + 1)
                act.activation(d, d, ACT.Abs)
                act.drain()
                act.activation(d, d, ACT.Relu, scale=-1.0, bias=1.0).then_inc(bx_made, 1)

            def split_z(g, b, par):
                if g % 6 == 0 and not first(b):
                    act.wait_ge(sz_done, UNITS * (b - 1) + 6 * (last_use(g // 6) + 1))
                act.wait_ge(z_ps, UNITS * b + g + 1)
                act.copy(z_piece(zh, g, par), zps[:, g % 2, 0:KO // 2]).then_inc(z_hi, 1)

            def far_pass(b, par, more):
                act.wait_ge(sz_done, UNITS * (b + 1))
                act.wait_ge(yt_ps, 4 * (b + 1))

                def first_chunks(n):
                    for g in range(AHEAD):
                        act.wait_ge(fz_ps, FAR_Z * b + n + g + 1)
                        act.copy(z_piece(zh, g, 1 - par), zps[:, g % 2, 0:KO // 2]).then_inc(fz_hi, 1)

                if more:
                    first_chunks(0)
                for t in range(TILES):
                    for ky in range(3):
                        for v in far_of(t, ky):
                            act.wait_ge(fs_ps, FAR_UNITS * b + v + 1)
                            if v:
                                act.wait_ge(fsz_done, FAR_UNITS * b + v)
                            act.copy(sh[:, FAR_SLOT].rearrange("p k n -> p (k n)"), sps[v % 2][:, 0:3 * P])\
                               .then_inc(fs_hi, 1)
                    act.wait_ge(fsz_done, FAR_UNITS * b + far_end(t))
                    if t >= 4:
                        act.wait_ge(fyt_ps, TILES * b + t - 3)
                    act.copy(ypm[:, t % 4, 0:C], acc[:, 0:C])
                    act.copy(ypm[:, t % 4, C:2 * P], acc[:, P:C]).then_inc(fy_pm, 1)
                if more:
                    first_chunks(AHEAD)
                act.wait_ge(fyt_ps, TILES * (b + 1))

            def split_s(u, b):
                act.wait_ge(s_ps, UNITS * b + u + 1)
                if u >= S_RING or not first(b):
                    act.wait_ge(sz_done, UNITS * b + u - S_RING + 1)
                act.copy(sh[:, u % S_RING].rearrange("p k n -> p (k n)"), sps[u % 2][:, 0:3 * P]).then_inc(s_hi, 1)

            def part1(b, par, more):
                if first(b):
                    for g in range(AHEAD):
                        split_z(g, b, par)
                    split_s(0, b)
                    split_s(1, b)
                for u in range(UNITS):
                    if u + 2 < UNITS:
                        split_s(u + 2, b)
                    elif more:
                        split_s(u + 2 - UNITS, b + 1)
                    if u == 24:
                        flag = is_far(act, b, par)
                    if u % 12 == 4 and u < 36:
                        column_hats(u // 12 + 1, b, par)
                    if u % 6 == 5:
                        t = u // 6
                        act.wait_ge(sz_done, UNITS * b + u + 1)
                        if t >= 4 or not first(b):
                            act.wait_ge(yt_ps, 4 * b + t // 2 - 1)
                        act.copy(ypm[:, t % 4, 0:C], acc[:, 0:C])
                        act.copy(ypm[:, t % 4, C:2 * P], acc[:, P:C]).then_inc(y_pm, 1)
                    if u + AHEAD < UNITS:
                        split_z(u + AHEAD, b, par)
                    elif more:
                        split_z(u + AHEAD - UNITS, b + 1, 1 - par)
                    if more:
                        part0(u, b + 1, 1 - par)
                where_far(flag, act, b, par, more, far_pass, (fz_hi, FAR_Z), (fs_hi, FAR_UNITS), (fy_pm, TILES))

            images((part0, part1, lambda: None), act)

            act.wait_ge(bn_done, 1)

            def gelu_pair(r_, slot):
                act.wait_ge(f_loaded[slot], 128 * r_ + 128)
                for i in range(3):
                    m = i // 2
                    act.activation(fin_y[slot][i], fin_y[slot][i], ACT.Gelu, scale=ga[:, m:m + 1],
                                   bias=gb[:, m:m + 1]).then_inc(f_gelu, 1)

            all_pairs(act, gelu_pair)

        @block.vector
        def _(dve):
            dve.wait_ge(weights_in, 6 * 16)
            for i, stage in enumerate((off_stage, proj_stage)):
                dve.tensor_reduce(wmaxt[:, i:i + 1], stage, AX.XY, ALU.max, apply_absolute_value=True)
            dve.wait_ge(const_in, CONST_DMAS * 16)
            dve.tensor_scalar(cmid[:, :], cy_sb[:, 0:1], -CENTRE, None, ALU.add)
            dve.tensor_copy(eye16[:, :], eye32[:, :]).then_inc(dve_setup, 1)
            dve.drain()
            dve.tensor_scalar(wmax[:, :], wmaxt[:, :], 1e-30, 1e30, ALU.max, ALU.min).then_inc(dve_setup, 1)
            dve.wait_ge(pe_setup, 1)
            dve.tensor_reduce(wmaxt[:, :], yt[:, 0:2 * P].rearrange("p (i n) -> p i n", i=2), AX.X, ALU.max)
            dve.drain()
            dve.tensor_scalar(unscale[:, :].bitcast(I32), wmaxt[:, :].bitcast(I32), 0x7F800000, None,
                              ALU.bitwise_and)
            dve.drain()
            dve.reciprocal(scale[:, :], unscale[:, :])
            dve.drain()
            off3 = lambda i: off_stage[:, i].rearrange("p (k j) -> p k j", k=TAPS)
            splits = [(off_stage[:, i], off3(i), wof[:, i, :, 0], wof[:, i, :, 1], 0) for i in range(2)]
            splits += [(proj_stage[:, i], proj_stage[:, i], flat2(wpr_h)[:, i], flat2(wpr_l)[:, i], 1)
                       for i in range(2)]
            for stage, shaped, w_h, w_l, i in splits:
                dve.tensor_scalar(stage, stage, scale[:, i:i + 1], None, ALU.mult)
            dve.drain()
            for stage, shaped, w_h, w_l, i in splits:
                dve.tensor_copy(w_h, shaped)
            dve.drain()
            for stage, shaped, w_h, w_l, i in splits:
                ins = dve.tensor_tensor(w_l, shaped, w_h, ALU.subtract)
            ins.then_inc(dve_setup, 1)

            def weights_ready():
                dve.wait_ge(matrices_in, MATRIX_DMAS * 16)
                dve.wait_ge(dve_setup, 3)

            def channel_stats(q, src):
                i, half = divmod(q, 2)
                dve.bn_stats(stats[:, i, half], src[:, i, half * 512:half * 512 + 512])

            def channel_moments():
                dve.drain()
                for i in range(2):
                    dve.bn_aggr(mv[:, i], stats[:, i].rearrange("p a b -> p (a b)"))
                dve.drain()
                dve.tensor_tensor(msq[:, :], mv[:, :, 0], mv[:, :, 0], ALU.mult)
                dve.drain()
                dve.tensor_tensor(mv[:, :, 1], mv[:, :, 1], msq[:, :], ALU.add).then_inc(gn_stats, 1)

            def group_variance(n, b):
                dve.wait_ge(gn_group, 2 * b + n + 1)
                if n or not first(b):
                    dve.wait_ge(xn_hi, 4 * b + 2 * n)
                dve.tensor_copy(flat(gmv), l0[0][:, 0:4])
                dve.drain()
                dve.tensor_tensor(msq[:, :], gmv[:, :, 0], gmv[:, :, 0], ALU.mult)
                dve.drain()
                dve.scalar_tensor_tensor(out=gvar[:, :], in0=gmv[:, :, 1], scalar=GN_EPS, in1=msq[:, :],
                                         op0=ALU.add, op1=ALU.subtract).then_inc(gn_var, 1)

            def residue(i, lo, hi, n, b):
                dve.wait_ge(xn_hi, 4 * b + 2 * n + i + 1)
                dve.tensor_tensor(lo, xn[:, 0] if i == 0 else xn[CB:P, 1], hi, ALU.subtract).then_inc(xn_lo, 1)

            def move(k, b, par):
                rows = lambda v: v.rearrange("p (h w) -> p h w", w=W)
                src = rows(inner(x2[k], par))
                dve.tensor_copy(rows(inner(x2s[k], 0))[:, :, 1:W], src[:, :, 0:W - 1])
                dve.tensor_copy(rows(inner(x2s[k], 1))[:, :, 0:W - 1], src[:, :, 1:W])
                seam = rows(x2w[k][:, par])
                dve.tensor_copy(seam[:, 0:WRAP], src[:, H - WRAP:H])
                return dve.tensor_copy(seam[:, WRAP:2 * WRAP], src[:, 0:WRAP])

            def zero_outside(hat, rows, tiles):
                for t in tiles:
                    for ky in range(3):
                        above, below = outside(t, ky, rows)
                        k = t * TAPS + 3 * ky
                        if above:
                            dve.memset(hat[:, k:k + 3, 0:above], 0.0)
                        if below:
                            dve.memset(hat[:, k:k + 3, len(rows) - below:len(rows)], 0.0)

            def part0(u, b, par):
                if u < 3:
                    dve.wait_ge(x_loaded, 48 * b + 48)
                    channel_stats(u, xin)
                if u == 2:
                    channel_stats(3, xin)
                    channel_moments()
                if u == 4:
                    group_variance(0, b)
                if u == 8:
                    residue(0, xl_a[:, :], xh_a[:, :], 0, b)
                if u == 10:
                    residue(1, xhl_b[CB:P, :], xhl_b[CB:P, :], 0, b)
                if u == 16:
                    dve.wait_ge(gram_ps, b + 1)
                    dve.tensor_copy(gram[:, 0], l0[0][:, 0:C])
                    dve.tensor_copy(gram[0:CB, 1, P:C], l0[0][0:CB, C + P:2 * C]).then_inc(gram_sb, 1)
                if u == 18:
                    dve.wait_ge(log_ps, b + 1)
                    for m in range(2):
                        dve.tensor_reduce(nmax[0:ROWS[m], m:m + 1], l0[0][0:ROWS[m], m * C:(m + 1) * C], AX.X,
                                          ALU.max, negate=True)
                    dve.drain()
                    for m in range(2):
                        r = ROWS[m]
                        ins = dve.tensor_scalar(nmaxs[0:r, m:m + 1], nmax[0:r, m:m + 1], HEAD_SCALE, None, ALU.mult)
                    ins.then_inc(log_max, 1)
                if u == 20:
                    dve.wait_ge(prob_exp, b + 1)
                    for m in range(2):
                        dve.reciprocal(rinv[0:ROWS[m], m:m + 1], rsum[0:ROWS[m], m:m + 1])
                    dve.drain()
                    for m in range(2):
                        r = ROWS[m]
                        ins = dve.tensor_scalar(prob[0:r, m], prob[0:r, m], rinv[0:r, m:m + 1], None, ALU.mult)
                    ins.then_inc(prob_sb, 1)
                if u == 22:
                    dve.wait_ge(mt_hi, b + 1)
                    mt = l0[0][:, 0:2 * C].rearrange("p (m o) -> p m o", m=2)
                    dve.tensor_tensor(mt_l[:, :, 0:C], mt, mt_h[:, :, 0:C], ALU.subtract)
                    dve.tensor_tensor(mt_l[:, :, C:2 * P], mt[:, :, P:C], mt_h[:, :, C:2 * P], ALU.subtract)\
                       .then_inc(mt_lo, 1)
                if 23 <= u < 27:
                    q = u - 23
                    m, n = q // 2, slice(q % 2 * 512, q % 2 * 512 + 512)
                    dve.wait_ge(mx_ps, 4 * b + q + 1)
                    if q == 0 and not first(b):
                        dve.wait_ge(x1_stored, 32 * b)
                    dve.scalar_tensor_tensor(out=x1[:, m, n], in0=l0[(q + 1) % 2][:, :], scalar=bo[:, m:m + 1],
                                             in1=xin[:, m, n], op0=ALU.add, op1=ALU.add).then_inc(x1_sb, 1)
                    dve.wait_ge(x1_sb, 4 * b + q + 1)
                    channel_stats(q, x1)
                if u == 27:
                    channel_moments()
                if u == 28:
                    group_variance(1, b)
                if u == 32:
                    residue(0, inner(x2[1], par), inner(x2[0], par), 1, b)
                if u == 33:
                    if not first(b):
                        dve.wait_ge(off_ps, b)
                    move(0, b, par)
                if u == 34:
                    residue(1, inner(x2[2], par)[CB:P], inner(x2[2], par)[CB:P], 1, b)
                if u == 35:
                    dve.wait_ge(xn_lo, 4 * b + 4)
                    move(1, b, par)
                if u == 36:
                    move(2, b, par).then_inc(x2_moved, 1)
                if u == 40:
                    dve.wait_ge(off_ps, b + 1)
                    if not isinstance(b, int) or b >= 2:
                        dve.wait_ge(st_made, 24 * (b - 1))
                    halves = l0[1][:, 0:TILES * 2 * J].rearrange("p (t i j) -> p t i j", t=TILES, i=2)
                    dve.scalar_tensor_tensor(out=off[:, par], in0=halves[:, :, 0], scalar=unscale[:, 0:1],
                                             in1=boff[:, :, :], op0=ALU.mult, op1=ALU.add)
                    dve.drain()
                    dve.scalar_tensor_tensor(out=off[:, par], in0=halves[:, :, 1], scalar=unscale[:, 0:1],
                                             in1=off[:, par], op0=ALU.mult, op1=ALU.add)
                    dve.drain()
                    yx = off[:, par, :, 0:2 * TAPS]
                    dve.tensor_scalar(yx, yx, -MAX_OFF, MAX_OFF, ALU.max, ALU.min).then_inc(off_sb, 1)
                if u in (41, 44):
                    h = u // 44
                    dve.wait_ge(off_sb, b + 1)
                    dve.tensor_tensor(ay_half(h, par), spread(off[:, par, half_tiles(h, par), 0:TAPS], R),
                                      cy_sb[:, None, None, 0:R].broadcast_to([P, TILES // 2, TAPS, R]), ALU.add)\
                       .then_inc(dy_sb, 1)
                if u in (42, 46):
                    h = u // 46
                    dve.wait_ge(hat_act, 2 * b + h + 1)
                    tiles = half_tiles(h, par)
                    zero_outside(ay[:, par], NEAR_ROWS, [t for t in (0, TILES - 1) if tiles.start <= t < tiles.stop])
                    if h == 0:
                        dve.tensor_scalar(mask[:, par], mask[:, par], 1.0, None, ALU.add)
                    dve.drain()
                    dve.tensor_tensor(ay_half(h, par), ay_half(h, par), spread(mask[:, par, tiles], R), ALU.mult)\
                       .then_inc(hats, 1)

            def offset_distance(b, par):
                dve.wait_ge(off_sb, b + 1)
                dve.tensor_scalar(ypos[:, :, :], off[:, par, :, 0:TAPS], cmid[:, 0:1], None, ALU.add)
                dve.drain()
                dve.tensor_reduce(offmax[:, :], ypos[:, :, :], AX.XY, ALU.max,
                                  apply_absolute_value=True).then_inc(omax_sb, 1)

            def offset_flag(b, par):
                dve.wait_ge(omax_ps, b + 1)
                dve.tensor_reduce(offmaxg[:, :], yt[:, 0:P], AX.X, ALU.max)
                dve.drain()
                dve.tensor_scalar(far[:, par:par + 1], offmaxg[:, :], CENTRE, None, ALU.is_gt).then_inc(flag_sb, 1)

            def split_z(g, b, par):
                dve.wait_ge(z_hi, UNITS * b + g + 1)
                dve.tensor_tensor(z_piece(zl, g, par), zps[:, g % 2, 0:KO // 2], z_piece(zh, g, par), ALU.subtract)\
                   .then_inc(z_lo, 1)

            def split_s(u, b):
                dve.wait_ge(s_hi, UNITS * b + u + 1)
                one = lambda t: t[:, u % S_RING].rearrange("p k n -> p (k n)")
                dve.tensor_tensor(one(sl), sps[u % 2][:, 0:3 * P], one(sh), ALU.subtract).then_inc(s_lo, 1)

            def far_pass(b, par, more):
                n_rows = len(FAR_ROWS)
                rows4 = ayf.rearrange("p (t k) r -> p t k r", t=TILES)
                dve.tensor_tensor(rows4, spread(off[:, par, :, 0:TAPS], n_rows),
                                  cy_sb[:, None, None, R:R + n_rows].broadcast_to([P, TILES, TAPS, n_rows]),
                                  ALU.add)
                dve.drain()
                dve.scalar_tensor_tensor(out=ayf, in0=ayf, scalar=-1.0, in1=ayf, op0=ALU.mult, op1=ALU.min)
                dve.drain()
                dve.tensor_scalar(ayf, ayf, 1.0, 0.0, ALU.add, ALU.max)
                dve.drain()
                dve.tensor_tensor(rows4, rows4, spread(mask[:, par], n_rows), ALU.mult)
                dve.drain()
                zero_outside(ayf, FAR_ROWS, range(TILES))
                dve.drain()

                def first_chunks(n):
                    for g in range(AHEAD):
                        dve.wait_ge(fz_hi, FAR_Z * b + n + g + 1)
                        dve.tensor_tensor(z_piece(zl, g, 1 - par), zps[:, g % 2, 0:KO // 2],
                                          z_piece(zh, g, 1 - par), ALU.subtract).then_inc(fz_lo, 1)

                if more:
                    first_chunks(0)
                for t in range(TILES):
                    for ky in range(3):
                        v0 = far_of(t, ky)[0]
                        if v0:
                            dve.wait_ge(fs_ps, FAR_UNITS * b + v0)
                        k = t * TAPS + 3 * ky
                        for kx in range(3):
                            ins = dve.tensor_tensor(
                                sTf[:, kx].rearrange("p (r x) -> p r x", r=n_rows),
                                ayf[:, k + kx, :, None].broadcast_to([P, n_rows, W]),
                                bx[:, par, k + kx, None, :].broadcast_to([P, n_rows, W]), ALU.mult)
                        ins.then_inc(f_st, 1)
                        for v in far_of(t, ky):
                            dve.wait_ge(fs_hi, FAR_UNITS * b + v + 1)
                            one = lambda w: w[:, FAR_SLOT].rearrange("p k n -> p (k n)")
                            dve.tensor_tensor(one(sl), sps[v % 2][:, 0:3 * P], one(sh), ALU.subtract)\
                               .then_inc(fs_lo, 1)
                    dve.wait_ge(fyt_ps, TILES * b + t + 1)
                    for m in range(2):
                        y = ych[:, m, t * P:(t + 1) * P]
                        ins = dve.scalar_tensor_tensor(out=y, in0=yt[:, m * P:(m + 1) * P], scalar=unscale[:, 1:2],
                                                       in1=y, op0=ALU.mult, op1=ALU.add)
                    ins.then_inc(fy_ch, 1)
                if more:
                    first_chunks(AHEAD)
                dve.drain()
                for q in range(2):
                    y_stats(q, b, par)

            def scale_y(q, b, par):
                dve.wait_ge(yt_ps, 4 * b + q + 1)
                if q == 0 and not first(b):
                    dve.wait_ge(y_stored, 32 * b)
                n = tile_at(2 * q, par) * P
                for m in range(2):
                    ins = dve.tensor_scalar(ych[:, m, n:n + 2 * P], yt[:, m * 2 * P:(m + 1) * 2 * P],
                                            unscale[:, 1:2], pb[:, m:m + 1], ALU.mult, ALU.add)
                ins.then_inc(y_ch, 1)

            def y_stats(q, b, par):
                dve.wait_ge(y_ch, 4 * b + 2 * (q // 2) + 2)
                if q >= 2:
                    dve.wait_ge(fy_ch, TILES * (b + 1))
                n = tile_at(4 * (q // 2), par) * P
                ins = dve.bn_stats(ystats[:, q % 2, bass.ds(2 * b + q // 2, 1), :], ych[:, q % 2, n:n + N // 2])
                if q == 3:
                    ins.then_inc(y_final, 1)

            def part1(b, par, more):
                if first(b):
                    for g in range(AHEAD):
                        split_z(g, b, par)
                    split_s(0, b)
                    split_s(1, b)
                for u in range(UNITS):
                    if u + 2 < UNITS:
                        split_s(u + 2, b)
                    elif more:
                        split_s(u + 2 - UNITS, b + 1)
                    if u + AHEAD < UNITS:
                        split_z(u + AHEAD, b, par)
                    elif more:
                        split_z(u + AHEAD - UNITS, b + 1, 1 - par)
                    if u == 7:
                        offset_distance(b, par)
                    if u == 11:
                        offset_flag(b, par)
                    if u == 13:
                        flag = is_far(dve, b, par)
                    if 5 <= u < 7 and not first(b):
                        y_stats(u - 3, b - 1, 1 - par)
                    if u in (38, 39):
                        y_stats(u - 38, b, par)
                    if u % 12 == 7 and u > 12:
                        scale_y(u // 12 - 1, b, par)
                    if more:
                        part0(u, b + 1, 1 - par)
                scale_y(3, b, par)
                where_far(flag, dve, b, par, more, far_pass, (fz_lo, FAR_Z), (f_st, 3 * TILES), (fs_lo, FAR_UNITS),
                          (fy_ch, TILES))
                if not more:
                    y_stats(2, b, par)
                    y_stats(3, b, par)

            images((part0, part1, weights_ready), dve)

            dve.wait_ge(y_final, NB)
            for m in range(2):
                dve.bn_aggr(ymv[:, m], ystats[:, m].rearrange("p a b -> p (a b)"))
            dve.drain()
            dve.tensor_scalar(yvar[:, :], ymv[:, :, 1], BN_EPS, None, ALU.add).then_inc(bn_var, 1)
            dve.wait_ge(bn_rstd, 1)
            dve.tensor_tensor(ga[:, :], gam[:, :], yrstd[:, :], ALU.mult)
            dve.drain()
            dve.tensor_tensor(gmean[:, :], ymv[:, :, 0], ga[:, :], ALU.mult)
            dve.drain()
            dve.tensor_tensor(gb[:, :], bet[:, :], gmean[:, :], ALU.subtract).then_inc(bn_done, 1)

            def add_pair(r_, slot):
                for i in range(3):
                    dve.wait_ge(f_gelu, 3 * FIN * r_ + 3 * slot + i + 1)
                    dve.tensor_tensor(fin_y[slot][i], fin_y[slot][i], fin_x[slot][i], ALU.add).then_inc(f_sum, 1)

            all_pairs(dve, add_pair)

        @block.gpsimd
        def _(pool):
            pool.memset(mhalf[:, :], -0.5)
            pool.memset(minus[:, :], -1.0)
            for t in (*x2, *x2s):
                ins = pool.memset(t[:, :, :], 0.0)
            ins.then_inc(pool_setup, 1)
            pool.wait_ge(pool_setup, 1)
            pool.wait_ge(const_in, CONST_DMAS * 16)

            def group_rstd(n, b):
                pool.wait_ge(gn_var, 2 * b + n + 1)
                pool.tensor_tensor(rstd[:, :], gvar[:, :], mhalf[:, :], ALU.pow).then_inc(gn_rstd, 1)
                pool.wait_ge(gn_rstd, 2 * b + n + 1)
                pool.tensor_tensor(nbias[:, :], gmv[:, :, 0], rstd[:, :], ALU.mult).then_inc(gn_mean, 1)
                pool.wait_ge(gn_mean, 2 * b + n + 1)
                pool.tensor_tensor(nbias[:, :], nbias[:, :], minus[:, :], ALU.mult).then_inc(gn_bias, 1)

            def part0(u, b, par):
                if u == 5:
                    group_rstd(0, b)
                if u == 29:
                    group_rstd(1, b)
                if u == 41:
                    column_distance(0, b, par)

            def column_distance(q, b, par):
                if q == 0:
                    pool.wait_ge(off_sb, b + 1)
                n = tile_at(2 * q, par)
                pool.tensor_tensor(bx_part(q, par).rearrange("p (t k) n -> p t k n", t=2),
                                   spread(off[:, par, n:n + 2, TAPS:2 * TAPS], W),
                                   cx_sb[:, None, :, :].broadcast_to([P, 2, TAPS, W]), ALU.add).then_inc(dx_sb, 1)

            def part1(b, par, more):
                for p in range(3 * TILES):
                    t, ky = tile_at(p // 3, par), p % 3
                    if p % (3 * TILES // 2) == 0:
                        pool.wait_ge(hats, 2 * b + p // (3 * TILES // 2) + 1)
                    if p % 6 == 0:
                        pool.wait_ge(bx_made, 4 * b + p // 6 + 1)
                    if p >= ST_RING or not first(b):
                        pool.wait_ge(s_ps, UNITS * b + 2 * (p - ST_RING) + 2)
                    k = t * TAPS + 3 * ky
                    a = ay[:, par, k:k + 3, :, None].broadcast_to([P, 3, R, W])
                    x_ = bx[:, par, k:k + 3, None, :].broadcast_to([P, 3, R, W])
                    pool.tensor_tensor(sT[:, p % ST_RING].rearrange("p k (r x) -> p k r x", r=R), a, x_, ALU.mult)\
                        .then_inc(st_made, 1)
                    if p in (1, 4, 10):
                        column_distance((1, 4, 10).index(p) + 1, b, par)
                    if more:
                        for u in (2 * p - 4, 2 * p - 3):
                            part0(u, b + 1, 1 - par)

            images((part0, part1, lambda: None), pool)

            pool.wait_ge(bn_var, 1)
            pool.tensor_tensor(yrstd[:, :], yvar[:, :], mhalf[:, :], ALU.pow).then_inc(bn_rstd, 1)

            def store_pair(r_, slot):
                for i in range(3):
                    pool.wait_ge(f_sum, 3 * FIN * r_ + 3 * slot + i + 1)
                    y, q = fin_y[slot][i], FIN * r_ + slot
                    if i < 2:
                        pool.dma_start(out[2 * q + i, 0:P], y).then_inc(f_stored[slot], 16)
                    else:
                        for h in range(2):
                            pool.dma_start(out[2 * q + h, P:C], y[CB * h:CB * h + CB]).then_inc(f_stored[slot], 16)

            all_pairs(pool, store_pair)
            for slot in range(FIN):
                pool.wait_ge(f_stored[slot], 64 * (ROUNDS + (slot < PAIRS - ROUND_ENDS)))

    return nc


def kernel(x, L0_conv_w_qkv, L0_conv_w_out, L0_conv_b_out, L1_conv_proj_w, L1_conv_proj_b, L1_conv_off_w,
           L1_conv_off_b, L1_conv_mask_w, L1_conv_mask_b, L1_conv_gamma, L1_conv_beta):
    import concourse.bacc as bacc
    from concourse.bass_utils import run_bass_kernel_spmd as run

    x = np.asarray(x)
    nb = x.shape[0]
    w_qkv = np.asarray(L0_conv_w_qkv)
    w_off = np.asarray(L1_conv_off_w)
    taps_last = lambda w: np.transpose(w, (1, 2, 3, 0))
    w_27 = np.concatenate([w_off[0::2], w_off[1::2], np.asarray(L1_conv_mask_w)], axis=0)
    b_off = np.asarray(L1_conv_off_b)
    b_27 = np.concatenate([b_off[0::2], b_off[1::2], np.asarray(L1_conv_mask_b)], axis=0)
    avg, cy, cx, eye = coordinate_tables()
    arrays = {
        "x": x.reshape(nb, C, N),
        "w_qkT": w_qkv[0:2 * C].T,
        "w_v": w_qkv[2 * C:3 * C],
        "w_outT": np.asarray(L0_conv_w_out).T,
        "b_out": np.asarray(L0_conv_b_out),
        "w_off": taps_last(w_27).reshape(C, TAPS * J),
        "b_off": b_27,
        "w_proj": taps_last(np.asarray(L1_conv_proj_w)).reshape(C, TAPS * C),
        "proj_b": np.asarray(L1_conv_proj_b),
        "gamma": np.asarray(L1_conv_gamma),
        "beta": np.asarray(L1_conv_beta),
        "avg": avg, "cy": cy, "cx": cx, "eye": eye,
    }
    nc = bacc.Bacc("TRN2", target_bir_lowering=False, num_devices=1)
    arrays = {f"in_{k}": np.ascontiguousarray(v) for k, v in arrays.items()}
    args = [nc.dram_tensor(k, v.shape, mybir.dt.from_np(v.dtype), kind="ExternalInput").ap()
            for k, v in arrays.items()]
    args.append(nc.dram_tensor("out", (nb, C, N), F32, kind="ExternalOutput").ap())
    build(nc, *args)
    r = run(nc, [arrays], core_ids=[0])
    return r.results[0]["out"].reshape(nb, C, H, W)
```
